# Optimizing a Trainium2 kernel written in Bass

```python
import numpy as np
import jax
import jax.numpy as jnp

def _softmax(x, axis=-1):
    return jax.nn.softmax(x, axis=axis)

def _gelu(x):
    return jax.nn.gelu(x, approximate=True)

def _silu(x):
    return jax.nn.silu(x)

def _sigmoid(x):
    return jax.nn.sigmoid(x)

def _layernorm(x, axis=-1, eps=1e-05):
    m = jnp.mean(x, axis=axis, keepdims=True)
    v = jnp.var(x, axis=axis, keepdims=True)
    return (x - m) / jnp.sqrt(v + eps)

def _scatter_add(tgt, idx, src, axis=0):
    return tgt.at[idx].add(src)

def _segment_sum(src, seg, n):
    return jax.ops.segment_sum(src, seg, n)
kernel_name = 'mk_xattn_ffn_d2_seqx_r8_43cfa1'

def setup_inputs(seed: int=0):
    np.random.seed(seed)
    _w = jnp.asarray

    def _rec_inputs():
        import jax
        import jax.numpy as jnp
        _rk = jax.random.key(seed)
        x = 0.0003765 + 1 * jax.random.normal(jax.random.fold_in(_rk, 1), (16, 128, 128), jnp.float32)
        _lenS = 128 - jax.random.randint(jax.random.fold_in(_rk, 7), (16,), 0, max(1, 128 // 4) + 1, jnp.int32)
        _lenS2 = 77 - jax.random.randint(jax.random.fold_in(_rk, 8), (16,), 0, max(1, 77 // 4) + 1, jnp.int32)
        _ctx_1024P = jax.random.normal(jax.random.fold_in(_rk, 11), (16, 16, 128), jnp.float32)
        _ctx_1024c = jax.random.dirichlet(jax.random.fold_in(_rk, 511), 0.3 * jnp.ones((16,), jnp.float32), (16, 77))
        _ctx_1024t = jnp.einsum('bsk,bkd->bsd', _ctx_1024c, _ctx_1024P)
        _ctx_1024t = _ctx_1024t * jax.lax.rsqrt(jnp.mean(jnp.square(_ctx_1024t)) + 1e-12) * 0.953939
        ctx_1024 = -0.000292821 + 1.00034 * (_ctx_1024t + 0.3 * jax.random.normal(jax.random.fold_in(_rk, 611), (16, 77, 128), jnp.float32))
        _validS = jnp.arange(128)[None, :] < _lenS[:, None]
        _validS2 = jnp.arange(77)[None, :] < _lenS2[:, None]
        _causal = jnp.tril(jnp.ones((128, 128), dtype=bool))
        mask_Bx1xSxS2_ik1 = jnp.where(jnp.broadcast_to(_validS2[:, None, None, :], (16, 1, 128, 77)), 1, 0).astype(jnp.int32)
        mask_1x1xSxS2_if1 = jnp.where(jnp.ones((1, 1, 128, 77), dtype=bool), 1, 0).astype(jnp.int32)
        return (x, ctx_1024, mask_Bx1xSxS2_ik1, mask_1x1xSxS2_if1)
    x, ctx_1024, mask_Bx1xSxS2_ik1, mask_1x1xSxS2_if1 = _rec_inputs()

    def _L0_xattn_setup():
        import jax, jax.numpy as jnp
        import numpy as np
        EMBED = 128
        HEADS = 16
        HEAD_DIM = EMBED // HEADS
        key = jax.random.key(seed)
        ks = jax.random.split(key, 6)
        N, S, E = (2, 256, EMBED)
        value = jax.random.normal(ks[0], (N, S, E), dtype=jnp.float32)
        k = jax.random.normal(ks[1], (N, S, E), dtype=jnp.float32)
        q = jax.random.normal(ks[2], (N, S, E), dtype=jnp.float32)
        mask = jax.random.randint(ks[3], (N, 1, S, S), 0, 2, dtype=jnp.int32)
        W_fc = jax.random.normal(ks[4], (E, E), dtype=jnp.float32) * (1.0 / np.sqrt(E))
        b_fc = jax.random.normal(ks[5], (E,), dtype=jnp.float32) * 0.01
        return {'value': value, 'key': k, 'query': q, 'mask': mask, 'W_fc': W_fc, 'b_fc': b_fc}
    _L0_xattn_all = _L0_xattn_setup()
    _L0_xattn_in = {k: v for k, v in _L0_xattn_all.items() if k in ('W_fc', 'b_fc')}
    del _L0_xattn_all

    def _L0_ffn_setup():
        import jax, jax.numpy as jnp
        import numpy as np
        B, T, D, H, E = (4, 256, 128, 256, 8)
        TOP_K = int(E * 0.25)
        key = jax.random.key(seed)
        ks = jax.random.split(key, 6)
        x = jax.random.normal(ks[0], (B, T, D), dtype=jnp.float32)
        gate = jax.random.normal(ks[1], (D, E), dtype=jnp.float32)
        W1 = jax.random.normal(ks[2], (E, D, H), dtype=jnp.float32) * D ** (-0.5)
        b1 = jnp.zeros((E, H), dtype=jnp.float32)
        W2 = jax.random.normal(ks[3], (E, H, D), dtype=jnp.float32) * H ** (-0.5)
        b2 = jnp.zeros((E, D), dtype=jnp.float32)
        return {'x': x, 'gate': gate, 'W1': W1, 'b1': b1, 'W2': W2, 'b2': b2}
    _L0_ffn_all = _L0_ffn_setup()
    _L0_ffn_in = {k: v for k, v in _L0_ffn_all.items() if k in ('gate', 'W1', 'b1', 'W2', 'b2')}
    del _L0_ffn_all

    def _L1_xattn_setup():
        import jax, jax.numpy as jnp
        import numpy as np
        import math
        H = 16
        D_MODEL = 128
        B, S = (2, 256)
        key = jax.random.key(seed)
        ks = jax.random.split(key, 7)
        q = jax.random.normal(ks[0], (B, S, D_MODEL), dtype=jnp.float32)
        k = jax.random.normal(ks[1], (B, S, D_MODEL), dtype=jnp.float32)
        v = jax.random.normal(ks[2], (B, S, D_MODEL), dtype=jnp.float32)
        mask = jnp.ones((1, 1, S, S), dtype=jnp.int32)
        sc = 1.0 / math.sqrt(D_MODEL)
        W_Q = jax.random.normal(ks[3], (D_MODEL, D_MODEL), dtype=jnp.float32) * sc
        W_K = jax.random.normal(ks[4], (D_MODEL, D_MODEL), dtype=jnp.float32) * sc
        W_V = jax.random.normal(ks[5], (D_MODEL, D_MODEL), dtype=jnp.float32) * sc
        W_T = jax.random.normal(ks[6], (D_MODEL, D_MODEL), dtype=jnp.float32) * sc
        return {'q': q, 'k': k, 'v': v, 'mask': mask, 'W_Q': W_Q, 'W_K': W_K, 'W_V': W_V, 'W_T': W_T}
    _L1_xattn_all = _L1_xattn_setup()
    _L1_xattn_in = {k: v for k, v in _L1_xattn_all.items() if k in ('W_Q', 'W_K', 'W_V', 'W_T')}
    del _L1_xattn_all

    def _L1_ffn_setup():
        import jax, jax.numpy as jnp
        import numpy as np
        NUM_EXPERTS = 8
        N_EMBD = 128
        D_FF = 4 * N_EMBD
        B, S = (4, 256)
        key = jax.random.key(seed)
        ks = jax.random.split(key, 6)
        x = jax.random.normal(ks[0], (B, S, N_EMBD), dtype=jnp.float32)
        gate_w = jax.random.normal(ks[1], (N_EMBD, NUM_EXPERTS), dtype=jnp.float32) * 0.02
        w1 = jax.random.normal(ks[2], (NUM_EXPERTS, N_EMBD, D_FF), dtype=jnp.float32) * 0.02
        b1 = jnp.zeros((NUM_EXPERTS, D_FF), dtype=jnp.float32)
        w2 = jax.random.normal(ks[3], (NUM_EXPERTS, D_FF, N_EMBD), dtype=jnp.float32) * 0.02
        b2 = jnp.zeros((NUM_EXPERTS, N_EMBD), dtype=jnp.float32)
        return {'x': x, 'gate_w': gate_w, 'w1': w1, 'b1': b1, 'w2': w2, 'b2': b2}
    _L1_ffn_all = _L1_ffn_setup()
    _L1_ffn_in = {k: v for k, v in _L1_ffn_all.items() if k in ('gate_w', 'w1', 'b1', 'w2', 'b2')}
    del _L1_ffn_all
    return {'x': x, 'ctx_1024': ctx_1024, 'mask_Bx1xSxS2_ik1': mask_Bx1xSxS2_ik1, 'mask_1x1xSxS2_if1': mask_1x1xSxS2_if1, 'L0_xattn_W_fc': _L0_xattn_in['W_fc'], 'L0_xattn_b_fc': _L0_xattn_in['b_fc'], 'L0_ffn_gate': _L0_ffn_in['gate'], 'L0_ffn_W1': _L0_ffn_in['W1'], 'L0_ffn_b1': _L0_ffn_in['b1'], 'L0_ffn_W2': _L0_ffn_in['W2'], 'L0_ffn_b2': _L0_ffn_in['b2'], 'L1_xattn_W_Q': _L1_xattn_in['W_Q'], 'L1_xattn_W_K': _L1_xattn_in['W_K'], 'L1_xattn_W_V': _L1_xattn_in['W_V'], 'L1_xattn_W_T': _L1_xattn_in['W_T'], 'L1_ffn_gate_w': _L1_ffn_in['gate_w'], 'L1_ffn_w1': _L1_ffn_in['w1'], 'L1_ffn_b1': _L1_ffn_in['b1'], 'L1_ffn_w2': _L1_ffn_in['w2'], 'L1_ffn_b2': _L1_ffn_in['b2']}

def reference(x, ctx_1024, mask_Bx1xSxS2_ik1, mask_1x1xSxS2_if1, L0_xattn_W_fc, L0_xattn_b_fc, L0_ffn_gate, L0_ffn_W1, L0_ffn_b1, L0_ffn_W2, L0_ffn_b2, L1_xattn_W_Q, L1_xattn_W_K, L1_xattn_W_V, L1_xattn_W_T, L1_ffn_gate_w, L1_ffn_w1, L1_ffn_b1, L1_ffn_w2, L1_ffn_b2):
    import jax
    import jax.numpy as jnp

    def _L0_xattn_ref(value, key, query, mask, W_fc, b_fc):
        import jax, jax.numpy as jnp
        import numpy as np
        EMBED = 128
        HEADS = 16
        HEAD_DIM = EMBED // HEADS
        N, Sq, E = query.shape
        Sk = key.shape[1]
        Sv = value.shape[1]
        v = value.reshape(N, Sv, HEADS, HEAD_DIM)
        k = key.reshape(N, Sk, HEADS, HEAD_DIM)
        q = query.reshape(N, Sq, HEADS, HEAD_DIM)
        energy = jnp.einsum('nqhd,nkhd->nhqk', q, k)
        energy = jnp.where(mask == 0, jnp.float32(-1e+20), energy)
        attention = jax.nn.softmax(energy / jnp.sqrt(jnp.float32(E)), axis=3)
        out = jnp.einsum('nhql,nlhd->nqhd', attention, v).reshape(N, Sq, E)
        out = out @ W_fc.T + b_fc
        return out

    def _L0_ffn_ref(x, gate, W1, b1, W2, b2):
        import jax, jax.numpy as jnp
        import numpy as np
        B, T, D, H, E = (4, 256, 128, 256, 8)
        TOP_K = int(E * 0.25)
        raw_gate = jax.nn.softmax(jnp.einsum('btd,de->bte', x, gate), axis=-1)
        topk_scores, topk_idx = jax.lax.top_k(raw_gate, TOP_K)
        mask = jax.nn.one_hot(topk_idx, E, dtype=raw_gate.dtype).sum(axis=-2)
        gate_topk = mask * raw_gate
        gate_topk = gate_topk / jnp.maximum(gate_topk.sum(axis=-1, keepdims=True), 1e-12)
        h = jax.nn.relu(jnp.einsum('btd,edh->beth', x, W1) + b1[None, :, None, :])
        expert_out = jnp.einsum('beth,ehd->betd', h, W2) + b2[None, :, None, :]
        out = jnp.einsum('bte,betd->btd', gate_topk, expert_out)
        return out

    def _L1_xattn_ref(q, k, v, mask, W_Q, W_K, W_V, W_T):
        import jax, jax.numpy as jnp
        import numpy as np
        import math
        H = 16
        D_MODEL = 128
        B, S = (2, 256)

        def split_heads(x):
            Bq, Sq, Dq = x.shape
            return x.reshape(Bq, Sq, H, Dq // H).transpose(0, 2, 1, 3)
        Q = split_heads(q @ W_Q)
        K = split_heads(k @ W_K)
        V = split_heads(v @ W_V)
        d_k = Q.shape[-1]
        score = jnp.einsum('bhqd,bhkd->bhqk', Q, K) / math.sqrt(d_k)
        score = jnp.where(mask == 0, jnp.float32(-1000000000.0), score)
        attn = jax.nn.softmax(score, axis=-1)
        out = jnp.einsum('bhqk,bhkd->bhqd', attn, V)
        out = out.transpose(0, 2, 1, 3).reshape(q.shape[0], q.shape[1], D_MODEL)
        return out @ W_T

    def _L1_ffn_ref(x, gate_w, w1, b1, w2, b2):
        import jax, jax.numpy as jnp
        import numpy as np
        NUM_EXPERTS = 8
        N_EMBD = 128
        D_FF = 4 * N_EMBD
        B, S = (4, 256)
        Bb, Ss, D = x.shape
        x_flat = x.reshape(-1, D)
        router_logits = x_flat @ gate_w
        router_probs = jax.nn.softmax(router_logits, axis=-1)
        expert_idx = jnp.argmax(router_probs, axis=-1)
        expert_w = jnp.take_along_axis(router_probs, expert_idx[:, None], axis=1)[:, 0]
        out = jnp.zeros_like(x_flat)
        for e in range(NUM_EXPERTS):
            h = jax.nn.gelu(x_flat @ w1[e] + b1[e], approximate=False)
            y = h @ w2[e] + b2[e]
            sel = expert_idx == e
            out = out + jnp.where(sel, expert_w, 0.0)[:, None] * y
        return out.reshape(Bb, Ss, D)
    x = x + _L0_xattn_ref(ctx_1024, ctx_1024, _layernorm(x, axis=-1), mask_Bx1xSxS2_ik1, L0_xattn_W_fc, L0_xattn_b_fc)
    x = x + _L0_ffn_ref(_layernorm(x, axis=-1), L0_ffn_gate, L0_ffn_W1, L0_ffn_b1, L0_ffn_W2, L0_ffn_b2)
    x = x + _L1_xattn_ref(_layernorm(x, axis=-1), ctx_1024, ctx_1024, mask_1x1xSxS2_if1, L1_xattn_W_Q, L1_xattn_W_K, L1_xattn_W_V, L1_xattn_W_T)
    x = x + _L1_ffn_ref(_layernorm(x, axis=-1), L1_ffn_gate_w, L1_ffn_w1, L1_ffn_b1, L1_ffn_w2, L1_ffn_b2)
    return x

_drawn_inputs = setup_inputs


def setup_inputs(seed=0):
    import zlib

    import numpy as np

    out = dict(_drawn_inputs(seed))
    spreads = {'L0_ffn_b1': (0.0, 0.1),
     'L0_ffn_b2': (0.0, 0.1),
     'L1_ffn_b1': (0.0, 0.8),
     'L1_ffn_b2': (0.0, 0.649)}
    factors = {'L1_ffn_gate_w': 4.217, 'L1_ffn_w1': 8.0, 'L1_ffn_w2': 8.0}
    for name, (base, spread) in spreads.items():
        noise = np.random.default_rng([zlib.crc32(name.encode()), seed]).standard_normal(out[name].shape)
        drawn = base * np.exp(spread * noise) if base else spread * noise
        out[name] = jnp.asarray(drawn.astype(out[name].dtype))
    for name, factor in factors.items():
        out[name] = (out[name] * factor).astype(out[name].dtype)
    return out
```

```python
from contextlib import ExitStack

import concourse.bass as bass
from concourse import mybir

F32 = mybir.dt.float32
BF16 = mybir.dt.bfloat16
I32 = mybir.dt.int32
U32 = mybir.dt.uint32
ALU = mybir.AluOpType
ACT = mybir.ActivationFunctionType
AX_X = mybir.AxisListType.X

P = 128
NB = 16
D = 128
NH = 16
DH = D // NH
NK = 77
G = 4
J = NH // G
GK = J * NK
E = 8
QT = 4
REGION = NB * P + P
SPARE = E * REGION
NEG = -1e20
EPS = 1e-5
FF = (256, 512)
TOPK = (2, 1)
TILES = tuple(NB * k + E - 1 for k in TOPK)
SCALE = (float(D) ** -0.5, float(DH) ** -0.5)


def wait(eng, sem, value):
    if not isinstance(value, int) or value > 0:
        eng.wait_ge(sem, value)


def here(b):
    return not isinstance(b, int) or 0 <= b < NB


def build(nc, x, ctx_in, mask0, mask1, wfc, bfc, gate0, w1_0, b1_0, w2_0, b2_0,
          wq, wk, wv, wt, gate1, w1_1, b1_1, w2_1, b2_1, out):
    xs = nc.dram_tensor("sorted_rows", (SPARE + P, D), F32).ap()
    ys = nc.dram_tensor("sorted_outputs", (max(TILES) * P, D), F32).ap()
    with ExitStack() as stack:
        def sb(name, shape, dt=F32):
            return stack.enter_context(nc.sbuf_tensor(name, shape, dt))

        def pb(name, shape, dt=F32):
            return stack.enter_context(nc.psum_tensor(name, shape, dt))

        def sem(name):
            return stack.enter_context(nc.semaphore(name))

        X = sb("X", [P, NB, D])
        W1 = [sb(f"W1_{l}", [P, E * FF[l]]) for l in range(2)]
        W2 = [sb(f"W2_{l}", [P, E * FF[l]]) for l in range(2)]
        b1row = [sb(f"b1row{l}", [E, FF[l]]) for l in range(2)]
        b2row = [sb(f"b2row{l}", [E, D]) for l in range(2)]
        b1rem = [sb(f"b1rem{l}", [E, 2, FF[l]]) for l in range(2)]
        b2rem = [sb(f"b2rem{l}", [E, 2, D]) for l in range(2)]
        b1part = [sb(f"b1part{l}", [E, 3, FF[l]], BF16) for l in range(2)]
        b2part = [sb(f"b2part{l}", [E, 3, D], BF16) for l in range(2)]
        b1s = [sb(f"b1s{l}", [3, E * FF[l]], BF16) for l in range(2)]
        b2s = [sb(f"b2s{l}", [3, E * D], BF16) for l in range(2)]
        gate = [sb(f"gate{l}", [P, E]) for l in range(2)]
        wfc_sb = sb("wfc_sb", [P, D])
        wfcT = sb("wfcT", [P, D])
        wq_sb, wk_sb, wv_sb, wt_sb = (sb(n, [P, D]) for n in ("wq_sb", "wk_sb", "wv_sb", "wt_sb"))
        bfc_sb = sb("bfc_sb", [1, D])
        ident = sb("ident", [P, P])
        identb = sb("identb", [P, P], BF16)
        ones_f = sb("ones_f", [P, P])
        onesb = sb("onesb", [P, P], BF16)
        before = sb("before", [P, P], BF16)
        own_a = sb("own_a", [P, J])
        own = sb("own", [P, J])
        zeros = sb("zeros", [P, D])
        minus_half = sb("minus_half", [P, 1])
        region0 = sb("region0", [P, QT, E])
        revf = sb("revf", [P, QT, E])
        iot = sb("iot", [P, QT, E], I32)
        tile_no_i = sb("tile_no_i", [1, max(TILES), E - 1], I32)
        tile_no = sb("tile_no", [1, max(TILES), E - 1])
        mask0_sb = sb("mask0_sb", [P, NB, NK], I32)
        mask1_sb = sb("mask1_sb", [P, NK], I32)
        ctx = sb("ctx", [NK, QT, D])
        bias = sb("bias", [P, 2, NK], BF16)
        bias1 = sb("bias1", [P, NK], BF16)
        st1 = sb("st1", [P, 2, 6])
        mv1 = sb("mv1", [P, 4, 2])
        ve1 = sb("ve1", [P, 4])
        rstd1 = sb("rstd1", [P, 4])
        st2 = sb("st2", [P, 2, 6])
        mv2 = sb("mv2", [P, 4, 2])
        ve2 = sb("ve2", [P, 4])
        rstd2 = sb("rstd2", [P, 4])
        xn = sb("xn", [P, 2, D])
        xT = sb("xT", [P, 2, P])
        qTs = sb("qTs", [P, 2, P])
        cT = sb("cT", [P, 2, NK])
        KB = sb("KB", [P, 2, GK])
        VP = sb("VP", [NK, 2, G, 160])
        M = sb("M", [P, 2, 2 * J])
        SB = sb("SB", [P, 2, 2 * GK])
        PR = sb("PR", [P, 2, 2 * GK])
        PT = sb("PT", [NK, 2, NH * P])
        SUM = sb("SUM", [P, 2, NH])
        R = sb("R", [P, 2, D])
        RT = sb("RT", [P, 2, P])
        OT = sb("OT", [P, 2, P])
        XN2 = sb("XN2", [P, NB, D])
        xg = sb("xg", [P, 2, D])
        xgT = sb("xgT", [P, 2, P])
        LG = sb("LG", [P, QT, E])
        rmax = sb("rmax", [P, QT])
        rsub = sb("rsub", [P, QT, E])
        rexp = sb("rexp", [P, QT, E])
        rsum = sb("rsum", [P, QT])
        rrec = sb("rrec", [P, QT])
        prob = sb("prob", [P, QT, E])
        val = sb("val", [P, 2, QT])
        eq = sb("eq", [P, QT, E])
        rank = sb("rank", [P, QT, E])
        first = sb("first", [P, QT])
        OH = sb("OH", [P, 2, NB, E])
        prob2 = sb("prob2", [P, QT, E])
        gden = sb("gden", [P, QT])
        OHB = sb("OHB", [P, QT, E], BF16)
        ohsum = sb("ohsum", [P, E])
        OHacc = sb("OHacc", [P, E], BF16)
        pos = sb("pos", [P, QT, E])
        posk = sb("posk", [P, QT, E])
        POSF = sb("POSF", [P, 2, NB])
        IDX = [sb(f"IDX{l}", [P, 2, NB], I32) for l in range(2)]
        IDXG = [sb(f"IDXG{l}", [P, 2, NB], I32) for l in range(2)]
        GV = [sb(f"GV{l}", [P, 2, NB]) for l in range(2)]
        cnt = sb("cnt", [P, E])
        cnti = sb("cnti", [P, E], I32)
        nti = sb("nti", [P, E], I32)
        ntf = sb("ntf", [P, E])
        cum = sb("cum", [P, 4, 4 + E])
        ge = sb("ge", [1, max(TILES), E - 1])
        gen = sb("gen", [1, max(TILES), E - 1])
        tef = sb("tef", [1, max(TILES)])
        startf = sb("startf", [1, max(TILES)])
        validf = sb("validf", [1, max(TILES)])
        offf = sb("offf", [1, max(TILES)])
        rowf = sb("rowf", [1, max(TILES)])
        shift = sb("shift", [P, E])
        moved = sb("moved", [P, NB, E])
        movedr = sb("movedr", [P, NB])
        fillf = sb("fillf", [1, E])
        TE = [sb(f"TE{l}", [1, TILES[l]], I32) for l in range(2)]
        ROW = [sb(f"ROW{l}", [1, TILES[l]], I32) for l in range(2)]
        FILL = [sb(f"FILL{l}", [1, E], I32) for l in range(2)]
        xt = sb("xt", [P, 4, D])
        xtT = sb("xtT", [P, 2, P])
        H = sb("H", [P, 2, max(FF)])
        HT = sb("HT", [P, 2, max(FF)])
        Y = sb("Y", [P, 4, D])
        YG = sb("YG", [P, 4, 2, D])

        S = pb("S", [P, G, 512])
        PTp = pb("PTp", [P, 2, 512])
        A = pb("A", [P, 512])
        B = pb("B", [P, 512])

        names = ("w_ok wfc_ld mask_ld bias_ld bias_split bias_parts pool_chain ident_ok consts_ok "
                 "a_full a_read b_full b_read bias1_ok bias_ok vp_ok "
                 "combined comb_part st1_ok mv1_ok ve1_ok rstd1_ok xn_ok "
                 "s_ok m_ok sub_ok exp_ok sum_ok recip_ok pt_ok pt_used cT_ok pv_done "
                 "st2_ok mv2_ok ve2_ok rstd2_ok xn2_ok xg_ok r1 rexp_ok r2 r3  ohb_ok idx_ok tab tables_ok idxg_ok "
                 "scattered filled xtT_ok xtT_used h_ok h_used hT_ok hT_used y_ok y_used stored held").split()
        s = {n: sem(n) for n in names}
        ctx_ld = [sem(f"ctx_ld{i}") for i in range(4)]
        x_ld = [sem(f"x_ld{i}") for i in range(2)]
        xt_ld = [sem(f"xt_ld{i}") for i in range(4)]
        y_st = [sem(f"y_st{i}") for i in range(4)]
        gath = [sem(f"gath{i}") for i in range(4)]
        block = stack.enter_context(nc.Block())

        R1N, R2N, R3N, TABN = 2, (18, 9), (7, 4), (29, 25)
        W_ALL = 16 * (6 + 2 * (1 + E))
        FIRST, LAST = -2, NB + 4

        def over_batches(eng, l, body):
            for b in range(FIRST, 4):
                body(l, b, b % 4, b // 4)
            with eng.Fori(1, 3) as i:
                for k in range(4):
                    body(l, i * 4 + k, k, i)
            for b in range(12, LAST):
                body(l, b, b % 4, b // 4)

        def over_tiles(eng, l, body, lead, lag):
            n = TILES[l]
            top = (n - lead) // 4 * 4
            for r in range(-lead, 4):
                body(l, r, r % 4, r // 4)
            with eng.Fori(1, top // 4) as i:
                for k in range(4):
                    body(l, i * 4 + k, k, i)
            for r in range(top, n + lag):
                body(l, r, r % 4, r // 4)

        def tile_here(l, r):
            return not isinstance(r, int) or 0 <= r < TILES[l]

        T0 = (0, TILES[0])
        SLOT0 = ([0] * 4, [len(range(k, TILES[0], 4)) for k in range(4)])

        def a_uses(l, b):
            return ((["rT"] if here(b - 1) else []) + (["xT"] + ["q"] * l if here(b + 1) else [])
                    + (["gT"] if here(b - 2) else []))

        def b_uses(l, b):
            return ((["pv"] if here(b - 1) else []) + (["cT"] + ["kv"] * l if here(b + 1) else [])
                    + (["proj"] if here(b - 1) else []) + (["lg"] if here(b - 3) else [])
                    + (["prefix"] if b % 4 == 3 and 0 <= b - 7 < NB else []))

        def turn(uses, l, b, k, q, stage):
            def at(b):
                n = 1 if uses is a_uses else 0
                if l:
                    n += sum(len(uses(0, c)) for c in range(FIRST, LAST)) + (uses is b_uses)
                n += sum(len(uses(l, c)) for c in range(FIRST, b))
                return n + uses(l, b).index(stage) + 1
            if isinstance(b, int):
                return at(b)
            c = at(4 + k)
            d = at(8 + k) - c
            return q * d + (c - d)

        def a_turn(*x):
            return turn(a_uses, *x)

        def b_turn(*x):
            return turn(b_uses, *x)

        def counts_turn(l):
            return sum(len(b_uses(i, c)) + 0 for i in range(l + 1) for c in range(FIRST, LAST)) + l + 1

        @block.sync
        def _(sp):
            xv = x.rearrange("b p d -> p b d")
            sp.dma_start(X[:, 0:4, :], xv[:, 0:4, :]).then_inc(x_ld[0], 16)

            def load_ctx(l, b, k):
                n = NB * l + b
                wait(sp, s["cT_ok"], n - 3)
                wait(sp, s["vp_ok"], n - 3)
                sp.dma_start(ctx[:, k, :], ctx_in[b, :, :]).then_inc(ctx_ld[k], 16)

            for b in range(4):
                load_ctx(0, b, b)
            sp.dma_start(wfc_sb[:, :], wfc).then_inc(s["wfc_ld"], 16)
            sp.dma_start(bfc_sb[:, :], bfc.rearrange("(a d) -> a d", a=1)).then_inc(s["wfc_ld"], 16)
            sp.dma_start(mask0_sb[:, :, :], mask0.rearrange("b o q k -> q (b o) k")).then_inc(s["mask_ld"], 16)
            sp.dma_start(mask1_sb[:, :], mask1.rearrange("a o q k -> q (a o k)")).then_inc(s["mask_ld"], 16)
            sp.dma_start(X[:, 4:NB, :], xv[:, 4:NB, :]).then_inc(x_ld[1], 16)
            for dst, src in ((gate[0], gate0), (gate[1], gate1), (wq_sb, wq), (wk_sb, wk), (wv_sb, wv), (wt_sb, wt)):
                sp.dma_start(dst[:, :], src).then_inc(s["w_ok"], 16)
            for l, (b1, b2) in enumerate(((b1_0, b2_0), (b1_1, b2_1))):
                sp.dma_start(b1row[l][:, :], b1).then_inc(s["bias_ld"], 16)
                sp.dma_start(b2row[l][:, :], b2).then_inc(s["bias_ld"], 16)
            for l, (w1, w2) in enumerate(((w1_0, w2_0), (w1_1, w2_1))):
                sp.dma_start(W1[l][:, :].rearrange("p (e f) -> p e f", e=E),
                             w1.rearrange("e d f -> d e f")).then_inc(s["w_ok"], 16)
                for e in range(E):
                    sp.dma_start(W2[l][:, e * FF[l]:(e + 1) * FF[l]].rearrange("p (c d) -> p c d", d=D),
                                 w2[e, :, :].rearrange("(c p) d -> p c d", p=P)).then_inc(s["w_ok"], 16)
            sp.wait_ge(s["bias_split"], 1)
            for l in range(2):
                for i in range(3):
                    sp.dma_start(b1s[l][i:i + 1, :].rearrange("p (e f) -> p e f", e=E),
                                 b1part[l][:, i, :]).then_inc(s["bias_parts"], 16)
                    sp.dma_start(b2s[l][i:i + 1, :].rearrange("p (e f) -> p e f", e=E),
                                 b2part[l][:, i, :]).then_inc(s["bias_parts"], 16)
            for l in range(2):
                if l:
                    for b in range(4):
                        load_ctx(l, b, b)
                with sp.Fori(1, 4) as i:
                    for k in range(4):
                        load_ctx(l, i * 4 + k, k)
                sp.wait_ge(s["tables_ok"], l + 1)
                sp.wait_ge(s["consts_ok"], 1)
                for e in range(E):
                    row = sp.value_load(FILL[l][0:1, e:e + 1], min_val=0, max_val=SPARE)
                    sp.dma_start(xs[bass.ds(row, P), :], zeros[:, :]).then_inc(s["filled"], 16)
                sp.wait_ge(s["filled"], 16 * E * (l + 1))
                sp.wait_ge(s["scattered"], 16 * NB * (TOPK[0] + l * TOPK[1]))

                def tile(l, r, k, j):
                    m = T0[l] + r
                    if tile_here(l, r + 4):
                        wait(sp, s["xtT_ok"], m + 1)
                        row = sp.value_load(ROW[l][0:1, bass.ds(r + 4, 1)], min_val=0, max_val=SPARE)
                        sp.dma_start(xt[:, k, :], xs[bass.ds(row, P), :]).then_inc(xt_ld[k], 16)
                    if tile_here(l, r - 2):
                        sp.wait_ge(s["y_used"], m - 1)
                        sp.dma_start(ys[bass.ds((r - 2) * P, P), :], Y[:, (k - 2) % 4, :]).then_inc(y_st[(k - 2) % 4], 16)

                over_tiles(sp, l, tile, 4, 2)
            with sp.Fori(0, NB) as b:
                sp.wait_ge(s["combined"], b + (NB + 1))
                sp.dma_start(out[b, :, :], X[:, b, :]).then_inc(s["stored"], 16)
            sp.wait_ge(s["stored"], 16 * NB)

        @block.gpsimd
        def _(pool):
            count = [0]

            def link(ins):
                count[0] += 1
                ins.then_inc(s["pool_chain"], 1)
                pool.wait_ge(s["pool_chain"], count[0])

            link(pool.memset(ones_f[:, :], 1.0))
            link(pool.memset(minus_half[:, :], -0.5))
            pool.affine_select(out=ident[:, :], in_=ones_f[:, :], compare_op=ALU.is_equal, fill=0.0, base=0,
                               pattern=[[-1, P]], channel_multiplier=1).then_inc(s["ident_ok"], 1)
            pool.wait_ge(s["ident_ok"], 1)
            link(pool.tensor_copy(identb[:, :], ident[:, :]))
            for g in range(G):
                rows = slice(32 * g, 32 * g + 32)
                link(pool.affine_select(out=own_a[rows, :], in_=ones_f[rows, 0:J], compare_op=ALU.is_ge, fill=0.0,
                                        base=0, pattern=[[-DH, J]], channel_multiplier=1))
                link(pool.affine_select(out=own[rows, :], in_=own_a[rows, :], compare_op=ALU.is_ge, fill=0.0,
                                        base=DH - 1, pattern=[[DH, J]], channel_multiplier=-1))
            pool.wait_ge(s["mask_ld"], 32)
            pool.tensor_scalar(bias1[:, :], mask1_sb[:, :], 0.0, NEG, ALU.is_equal, ALU.mult).then_inc(s["bias1_ok"], 1)
            link(pool.memset(VP[:, :, :, :], 0.0))

            def constants():
                link(pool.memset(zeros[:, :], 0.0))
                link(pool.memset(OHacc[:, :], 0.0))
                link(pool.memset(cum[:, :, :], 0.0))
                link(pool.tensor_copy(onesb[:, :], ones_f[:, :]))
                link(pool.affine_select(out=before[:, :], in_=onesb[:, :], compare_op=ALU.is_gt, fill=0.0, base=0,
                                        pattern=[[1, P]], channel_multiplier=-1))
                link(pool.iota(iot[:, :, :], pattern=[[0, QT], [REGION, E]], base=0, channel_multiplier=0))
                link(pool.tensor_copy(region0[:, :, :], iot[:, :, :]))
                link(pool.iota(iot[:, :, :], pattern=[[0, QT], [-1, E]], base=E, channel_multiplier=0))
                link(pool.tensor_copy(revf[:, :, :], iot[:, :, :]))
                link(pool.iota(tile_no_i[:, :, :], pattern=[[1, max(TILES)], [0, E - 1]], base=0, channel_multiplier=0))
                pool.tensor_copy(tile_no[:, :, :], tile_no_i[:, :, :]).then_inc(s["consts_ok"], 1)

            def split_biases():
                pool.wait_ge(s["bias_ld"], 64)
                for l in range(2):
                    for row, rem, part in ((b1row[l], b1rem[l], b1part[l]), (b2row[l], b2rem[l], b2part[l])):
                        link(pool.tensor_copy(part[:, 0, :], row[:, :]))
                        link(pool.tensor_tensor(rem[:, 0, :], row[:, :], part[:, 0, :], ALU.subtract))
                        link(pool.tensor_copy(part[:, 1, :], rem[:, 0, :]))
                        link(pool.tensor_tensor(rem[:, 1, :], rem[:, 0, :], part[:, 1, :], ALU.subtract))
                        link(pool.tensor_copy(part[:, 2, :], rem[:, 1, :]))
                pool.sem_inc(s["bias_split"], 1)

            def rstd(n, k, mv, ve, rs, mv_ok, ve_ok, rs_ok):
                pool.wait_ge(s[mv_ok], n + 1)
                pool.tensor_scalar(ve[:, k:k + 1], mv[:, k, 1:2], EPS, None, ALU.add).then_inc(s[ve_ok], 1)
                pool.wait_ge(s[ve_ok], n + 1)
                pool.tensor_tensor(rs[:, k:k + 1], ve[:, k:k + 1], minus_half[:, :], ALU.pow).then_inc(s[rs_ok], 1)

            def body(l, b):
                n = NB * l + b
                if l == 0 and here(b + 1):
                    k, p = (b + 1) % 4, (b + 1) % 2
                    pool.wait_ge(ctx_ld[k], 16 * ((b + 1) // 4 + 1))
                    wait(pool, s["pv_done"], n)
                    for g in range(G):
                        v = pool.tensor_copy(VP[:, p, g, :].rearrange("k (j c) -> k j c", c=40)[:, :, 0:DH],
                                             ctx[:, k, 32 * g:32 * g + 32].rearrange("k (j c) -> k j c", c=DH))
                    v.then_inc(s["vp_ok"], 1)
                    wait(pool, s["s_ok"], 2 * n)
                    pool.tensor_scalar(bias[:, p, :], mask0_sb[:, b + 1, :], 0.0, NEG, ALU.is_equal,
                                       ALU.mult).then_inc(s["bias_ok"], 1)
                if here(b - 1):
                    wait(pool, s["xg_ok"], n - 4)
                    rstd(n - 1, (b - 1) % 4, mv2, ve2, rstd2, "mv2_ok", "ve2_ok", "rstd2_ok")
                if here(b + 2):
                    wait(pool, s["xn_ok"], n - 1)
                    rstd(n + 2, (b + 2) % 4, mv1, ve1, rstd1, "mv1_ok", "ve1_ok", "rstd1_ok")
                if here(b - 8):
                    t = b - 8
                    pool.wait_ge(s["idx_ok"], 4 * l + t // 4 + 1)
                    pool.wait_ge(s["xn2_ok"], NB * l + t + 1)
                    for k in range(TOPK[l]):
                        pool.indirect_dma_start(
                            out=xs, out_offset=bass.IndirectOffsetOnAxis(ap=IDX[l][:, k, t:t + 1].bitcast(U32), axis=0),
                            in_=XN2[:, t, :], in_offset=None).then_inc(s["scattered"], 16)

            def gather(l, t):
                wait(pool, s["combined"], NB * l + t - 3)
                for k in range(TOPK[l]):
                    pool.indirect_dma_start(
                        out=YG[:, t % 4, k, :], out_offset=None, in_=ys,
                        in_offset=bass.IndirectOffsetOnAxis(ap=IDXG[l][:, k, t:t + 1].bitcast(U32), axis=0),
                    ).then_inc(gath[t % 4], 16)

            for l in range(2):
                for b in range(FIRST, NB + 8):
                    if l and b == FIRST:
                        for t in range(4):
                            gather(0, t)
                    body(l, b)
                    if l == 0 and b == 0:
                        constants()
                    if l == 0 and b == 1:
                        split_biases()
                    if l and 4 <= b + 6 < NB:
                        gather(0, b + 6)
                pool.wait_ge(s["idxg_ok"], l + 1)
                for k in range(4):
                    pool.wait_ge(y_st[k], 16 * sum(len(range(k, TILES[i], 4)) for i in range(l + 1)))
            for t in range(NB):
                gather(1, t)

        @block.scalar
        def _(act):
            def exps(l, n, h):
                wait(act, s["sub_ok"], 2 * n + h + 1)
                wait(act, s["sum_ok"], 2 * n + h - 1)
                wait(act, s["pt_ok"], 4 * n + 2 * h - 2)
                act.activation(PR[:, h, :], SB[:, h, :], ACT.Exp, scale=SCALE[l]).then_inc(s["exp_ok"], 1)

            def probs_out(n, p, h):
                wait(act, s["pv_done"], n - 1)
                for q in range(2):
                    wait(act, s["pt_ok"], 4 * n + 2 * h + q + 1)
                    at = (2 * h + q) * J * P
                    act.copy(PT[:, p, at:at + J * P], PTp[0:NK, q, :]).then_inc(s["pt_used"], 1)

            def from_a(dst, cols, t):
                act.wait_ge(s["a_full"], t)
                act.copy(dst, A[:, cols:cols + P]).then_inc(s["a_read"], 1)

            def body(l, b, k, q):
                n, p, at = NB * l + b, k % 2, (l, b, k, q)
                if here(b):
                    exps(l, n, 1)
                    probs_out(n, p, 0)
                if here(b - 1):
                    from_a(RT[:, 1 - p, :], 0, a_turn(*at, "rT"))
                if here(b + 1):
                    wait(act, s["s_ok"], 2 * n)
                    from_a(xT[:, 1 - p, :], 128, a_turn(*at, "xT"))
                    if l:
                        from_a(qTs[:, 1 - p, :], 256, a_turn(*at, "q"))
                    exps(l, n + 1, 0)
                if here(b):
                    probs_out(n, p, 1)
                if here(b - 2):
                    from_a(xgT[:, p, :], 384, a_turn(*at, "gT"))
                if k == 2 and here(b - 6):
                    act.wait_ge(s["r1"], 2 * (4 * l + q - 1) + 2)
                    act.activation(rexp[:, :, :], rsub[:, :, :], ACT.Exp).then_inc(s["rexp_ok"], 1)

            from_a(wfcT[:, :], 0, 1)
            for l in range(2):
                over_batches(act, l, body)

                def tile(l, r, k, j):
                    m = T0[l] + r
                    if tile_here(l, r + 1):
                        act.wait_ge(s["h_ok"], m + 2)
                        wait(act, s["hT_ok"], m)
                        act.activation(H[:, (k + 1) % 2, 0:FF[l]], S[:, (k + 1) % 2, 0:FF[l]],
                                       ACT.Gelu if l else ACT.Relu).then_inc(s["h_used"], 1)
                    if tile_here(l, r + 2):
                        act.wait_ge(s["xtT_ok"], m + 3)
                        wait(act, s["h_ok"], m + 1)
                        act.copy(xtT[:, k % 2, :], A[:, 0:P]).then_inc(s["xtT_used"], 1)

                over_tiles(act, l, tile, 2, 0)

        @block.tensor
        def _(pe):
            mm = pe.matmul

            def scores(l, b, k, q, h):
                n, p = NB * l + b, k % 2
                made = (l, b - 1, (k - 1) % 4, q if k else (q - 1))
                pe.wait_ge(s["a_read"], a_turn(*made, "q" if l else "xT"))
                pe.wait_ge(s["b_read"], b_turn(*made, "kv" if l else "cT"))
                if l:
                    pe.wait_ge(s["bias1_ok"], 1)
                else:
                    pe.wait_ge(s["bias_ok"], n + 1)
                wait(pe, s["sub_ok"], 2 * n + h - 1)
                queries = qTs if l else xT
                mask = bias1[:, :] if l else bias[:, p, :]
                for g in (2 * h, 2 * h + 1):
                    rows = slice(32 * g, 32 * g + 32)
                    mm(S[:, g, 0:GK], queries[rows, p, :], KB[rows, p, :], start=True, stop=False)
                for g in (2 * h, 2 * h + 1):
                    last = mm(S[:, g, 0:GK].rearrange("p (j k) -> p j k", j=J), identb[:, :],
                              mask[:, None, :].to_broadcast([P, J, NK]), start=False, stop=True)
                last.then_inc(s["s_ok"], 1)

            def probs_t(n, h):
                pe.wait_ge(s["exp_ok"], 2 * n + h + 1)
                for q in range(2):
                    wait(pe, s["pt_used"], 4 * n + 2 * h + q - 1)
                    for j in range(J):
                        at = (q * J + j) * NK
                        t = pe.transpose(PTp[0:NK, q, j * P:(j + 1) * P], PR[:, h, at:at + NK], ident[:, :])
                    t.then_inc(s["pt_ok"], 1)

            def fill(full, read, t):
                wait(pe, s[read], t - 1)

            def body(l, b, k, q):
                n, p, at = NB * l + b, k % 2, (l, b, k, q)
                if here(b):
                    scores(*at, 1)
                    probs_t(n, 0)
                if here(b - 1):
                    pe.wait_ge(s["pt_used"], 4 * n)
                    pe.wait_ge(s["vp_ok"], n)
                    fill("b_full", "b_read", b_turn(*at, "pv"))
                    for j in range(J):
                        for g in range(G):
                            v = mm(B[32 * g:32 * g + 32, 0:P], VP[:, 1 - p, g, 32 * j:32 * j + 32],
                                   PT[:, 1 - p, (g * J + j) * P:(g * J + j + 1) * P], start=(j == 0), stop=(j == J - 1))
                    v.then_inc(s["b_full"], 1)
                    pe.wait_ge(s["recip_ok"], n)
                    fill("a_full", "a_read", a_turn(*at, "rT"))
                    pe.transpose(A[:, 0:P], R[:, 1 - p, :], ident[:, :]).then_inc(s["a_full"], 1)
                if here(b + 1):
                    pe.wait_ge(s["xn_ok"], n + 2)
                    fill("a_full", "a_read", a_turn(*at, "xT"))
                    pe.transpose(A[:, 128:256], xn[:, 1 - p, :], ident[:, :]).then_inc(s["a_full"], 1)
                    pe.wait_ge(ctx_ld[(k + 1) % 4], 16 * (4 * l + q + (k + 1) // 4 + 1))
                    fill("b_full", "b_read", b_turn(*at, "cT"))
                    pe.transpose(B[:, 128:128 + NK], ctx[:, (k + 1) % 4, :], ident[0:NK, 0:NK]).then_inc(s["b_full"], 1)
                    if l:
                        pe.wait_ge(s["a_read"], a_turn(*at, "xT"))
                        pe.wait_ge(s["w_ok"], W_ALL)
                        mm(A[:, 256:384], wq_sb[:, :], xT[:, 1 - p, :], start=True, stop=True).then_inc(s["a_full"], 1)
                        pe.wait_ge(s["b_read"], b_turn(*at, "cT"))
                        mm(B[:, 256:256 + NK], wk_sb[:, :], cT[:, 1 - p, :], start=True, stop=True)
                        mm(B[0:NK, 384:512], cT[:, 1 - p, :], wv_sb[:, :], start=True, stop=True).then_inc(s["b_full"], 1)
                    nk, nq = (k + 1) % 4, q + (k + 1) // 4
                    scores(l, b + 1, nk, nq, 0)
                if here(b):
                    probs_t(n, 1)
                if here(b - 1):
                    pe.wait_ge(s["b_read"], b_turn(*at, "pv"))
                    fill("b_full", "b_read", b_turn(*at, "proj"))
                    if l == 0:
                        mm(B[:, 256:384], ones_f[0:1, :], bfc_sb[0:1, :], start=True, stop=False)
                    mm(B[:, 256:384], OT[:, 1 - p, :], wt_sb[:, :] if l else wfcT[:, :],
                       start=bool(l), stop=True).then_inc(s["b_full"], 1)
                if here(b - 3):
                    prev = (l, b - 1, (k - 1) % 4, q if k else q - 1)
                    pe.wait_ge(s["w_ok"], W_ALL)
                    pe.wait_ge(s["a_read"], a_turn(*prev, "gT"))
                    fill("b_full", "b_read", b_turn(*at, "lg"))
                    mm(B[:, 384:384 + E], xgT[:, 1 - p, :], gate[l][:, :], start=True, stop=True).then_inc(s["b_full"], 1)
                if here(b - 2):
                    pe.wait_ge(s["xg_ok"], n - 1)
                    fill("a_full", "a_read", a_turn(*at, "gT"))
                    pe.transpose(A[:, 384:512], xg[:, p, :], ident[:, :]).then_inc(s["a_full"], 1)
                if k == 3 and here(b - 7):
                    quad = 4 * l + q - 1
                    pe.wait_ge(s["ohb_ok"], quad + 1)
                    wait(pe, s["consts_ok"], 1)
                    fill("b_full", "b_read", b_turn(*at, "prefix"))
                    mm(B[:, 0:QT * E], before[:, :], OHB[:, :, :], start=True, stop=False)
                    for d in range(1, QT):
                        mm(B[:, d * E:QT * E], onesb[:, :], OHB[:, 0:QT - d, :], start=False, stop=False)
                    mm(B[:, 0:QT * E].rearrange("p (t e) -> p t e", t=QT), onesb[:, :],
                       OHacc[:, None, :].to_broadcast([P, QT, E]), start=False, stop=True).then_inc(s["b_full"], 1)

            pe.wait_ge(s["wfc_ld"], 32)
            pe.wait_ge(s["ident_ok"], 1)
            pe.transpose(A[:, 0:P], wfc_sb[:, :], ident[:, :]).then_inc(s["a_full"], 1)
            for l in range(2):
                over_batches(pe, l, body)
                pe.wait_ge(s["r3"], R3N[0] * 4 + l * R3N[1] * 4)
                fill("b_full", "b_read", counts_turn(l))
                mm(B[:, 0:E], onesb[:, :], OHacc[:, :], start=True, stop=True).then_inc(s["b_full"], 1)
                pe.wait_ge(s["tables_ok"], l + 1)
                pe.wait_ge(s["bias_parts"], 16 * 12)
                nf = FF[l] // P

                def tile(l, r, k, j):
                    m = T0[l] + r
                    if tile_here(l, r + 1):
                        e = pe.value_load(TE[l][0:1, bass.ds(r + 1, 1)], min_val=0, max_val=E - 1)
                        pe.wait_ge(s["xtT_used"], m + 2)
                        wait(pe, s["h_used"], m)
                        h = S[:, (k + 1) % 2, 0:FF[l]]
                        mm(h, onesb[0:3, :], b1s[l][:, bass.ds(e * FF[l], FF[l])], start=True, stop=False)
                        mm(h, xtT[:, (k + 1) % 2, :], W1[l][:, bass.ds(e * FF[l], FF[l])],
                           start=False, stop=True).then_inc(s["h_ok"], 1)
                    if tile_here(l, r - 1):
                        e = pe.value_load(TE[l][0:1, bass.ds(r - 1, 1)], min_val=0, max_val=E - 1)
                        pe.wait_ge(s["hT_used"], m)
                        wait(pe, s["y_used"], m - 2)
                        y = PTp[:, (k + 1) % 2, 0:D]
                        mm(y, onesb[0:3, :], b2s[l][:, bass.ds(e * D, D)], start=True, stop=False)
                        for c in range(nf):
                            v = mm(y, HT[:, (k + 1) % 2, c * P:(c + 1) * P], W2[l][:, bass.ds(e * FF[l] + c * P, D)],
                                   start=False, stop=(c == nf - 1))
                        v.then_inc(s["y_ok"], 1)
                    if tile_here(l, r):
                        pe.wait_ge(s["h_used"], m + 1)
                        wait(pe, s["hT_used"], m - 1)
                        for c in range(nf):
                            v = pe.transpose(S[:, 2 + k % 2, c * P:(c + 1) * P], H[:, k % 2, c * P:(c + 1) * P], ident[:, :])
                        v.then_inc(s["hT_ok"], 1)
                    if tile_here(l, r + 2):
                        kk = (k + 2) % 4
                        pe.wait_ge(xt_ld[kk], (j + (k + 2) // 4 + SLOT0[l][kk] + 1) * 16)
                        wait(pe, s["xtT_used"], m + 2)
                        pe.transpose(A[:, 0:P], xt[:, kk, :], ident[:, :]).then_inc(s["xtT_ok"], 1)

                over_tiles(pe, l, tile, 2, 1)
                done = T0[l] + TILES[l]
                for name in ("hT_used", "h_used", "y_used", "xtT_used"):
                    pe.wait_ge(s[name], done)

        @block.vector
        def _(dve):
            tt, ts, cp = dve.tensor_tensor, dve.tensor_scalar, dve.tensor_copy

            def halves(h):
                return S[:, 2 * h:2 * h + 2, 0:GK].rearrange("p g (j k) -> p g j k", j=J)

            def max_sub(n, h):
                dve.wait_ge(s["s_ok"], 2 * n + h + 1)
                wait(dve, s["exp_ok"], 2 * n + h - 1)
                m = M[:, h, :].rearrange("p (g j) -> p g j", g=2)
                dve.tensor_reduce(m, halves(h), AX_X, ALU.max).then_inc(s["m_ok"], 1)
                dve.wait_ge(s["m_ok"], 2 * n + h + 1)
                tt(SB[:, h, :].rearrange("p (g j k) -> p g j k", g=2, j=J), halves(h),
                   m[:, :, :, None].to_broadcast([P, 2, J, NK]), ALU.subtract).then_inc(s["sub_ok"], 1)

            def sums(n, p, h):
                dve.wait_ge(s["exp_ok"], 2 * n + h + 1)
                dve.tensor_reduce(SUM[:, p, 8 * h:8 * h + 8], PR[:, h, :].rearrange("p (j k) -> p j k", k=NK),
                                  AX_X, ALU.add).then_inc(s["sum_ok"], 1)

            def hold():
                dve.sem_inc(s["held"], 1)

            def stats(src, n, p, k, st, mv, st_ok, mv_ok):
                hold()
                dve.bn_stats(st[:, p, :], src).then_inc(s[st_ok], 1)
                dve.wait_ge(s[st_ok], n + 1)
                hold()
                dve.bn_aggr(mv[:, k, :], st[:, p, :]).then_inc(s[mv_ok], 1)

            def combine(l, b, k, q):
                dve.wait_ge(gath[k], (TOPK[l] * (q + 1) + l * TOPK[0] * 4) * 16)
                for c in range(TOPK[l]):
                    lastc = c == TOPK[l] - 1
                    if c:
                        dve.wait_ge(s["comb_part"], b + 1)
                    dve.scalar_tensor_tensor(out=X[:, b, :], in0=YG[:, k, c, :], scalar=GV[l][:, c, bass.ds(b, 1)],
                                             in1=X[:, b, :], op0=ALU.mult, op1=ALU.add)\
                        .then_inc(s["combined" if lastc else "comb_part"], 1)

            def chain(name, base):
                count = [0]

                def link(ins):
                    count[0] += 1
                    ins.then_inc(s[name], 1)
                    dve.wait_ge(s[name], base + count[0])
                return link, count

            def route1(l, quad):
                link, c = chain("r1", quad * R1N)
                link(dve.tensor_reduce(rmax[:, :], LG[:, :, :], AX_X, ALU.max))
                link(tt(rsub[:, :, :], LG[:, :, :], rmax[:, :, None].to_broadcast([P, QT, E]), ALU.subtract))
                assert c[0] == R1N

            def over_e(v):
                return v[:, :, None].to_broadcast([P, QT, E])

            def route2(l, quad, t0):
                def oh(k):
                    return OH[:, k, bass.ds(t0, QT), :]
                link, c = chain("r2", quad * R2N[l] if l == 0 else (quad - 4) * R2N[1] + 4 * R2N[0])
                dve.wait_ge(s["rexp_ok"], quad + 1)
                link(dve.tensor_reduce(rsum[:, :], rexp[:, :, :], AX_X, ALU.add))
                link(dve.reciprocal(rrec[:, :], rsum[:, :]))
                link(tt(prob[:, :, :], rexp[:, :, :], over_e(rrec), ALU.mult))
                for k in range(TOPK[l]):
                    pk = prob if k == 0 else prob2
                    if k:
                        link(dve.scalar_tensor_tensor(out=prob2[:, :, :], in0=oh(0), scalar=-2.0,
                                                      in1=prob[:, :, :], op0=ALU.mult, op1=ALU.add))
                    link(dve.tensor_reduce(val[:, k, :], pk[:, :, :], AX_X, ALU.max))
                    link(tt(eq[:, :, :], pk[:, :, :], over_e(val[:, k, :]), ALU.is_equal))
                    link(tt(rank[:, :, :], eq[:, :, :], revf[:, :, :], ALU.mult))
                    link(dve.tensor_reduce(first[:, :], rank[:, :, :], AX_X, ALU.max))
                    link(tt(oh(k), revf[:, :, :], over_e(first), ALU.is_equal))
                if TOPK[l] == 2:
                    tt(OHB[:, :, :], oh(0), oh(1), ALU.add).then_inc(s["ohb_ok"], 1)
                    link(tt(gden[:, :], val[:, 0, :], val[:, 1, :], ALU.add))
                    link(ts(gden[:, :], gden[:, :], 1e-12, None, ALU.max))
                    link(dve.reciprocal(gden[:, :], gden[:, :]))
                    link(tt(GV[l][:, :, bass.ds(t0, QT)], val[:, :, :], gden[:, None, :].to_broadcast([P, 2, QT]), ALU.mult))
                else:
                    ts(OHB[:, :, :], oh(0), 1.0, None, ALU.mult).then_inc(s["ohb_ok"], 1)
                    link(ts(GV[l][:, 0, bass.ds(t0, QT)], val[:, 0, :], 1.0, None, ALU.mult))
                assert c[0] == R2N[l], c

            def route3(l, quad, t0, turn_no):
                link, c = chain("r3", quad * R3N[0] if l == 0 else (quad - 4) * R3N[1] + 4 * R3N[0])
                dve.wait_ge(s["b_full"], turn_no)
                tt(pos[:, :, :], B[:, 0:QT * E].rearrange("p (t e) -> p t e", t=QT), region0[:, :, :],
                   ALU.add).then_inc(s["b_read"], 1)
                dve.wait_ge(s["b_read"], turn_no)
                for k in range(TOPK[l]):
                    link(tt(posk[:, :, :], pos[:, :, :], OH[:, k, bass.ds(t0, QT), :], ALU.mult))
                    link(dve.tensor_reduce(POSF[:, k, bass.ds(t0, QT)], posk[:, :, :], AX_X, ALU.add))
                    ins = ts(IDX[l][:, k, bass.ds(t0, QT)], POSF[:, k, bass.ds(t0, QT)], 1.0, None, ALU.mult)
                    if k == TOPK[l] - 1:
                        ins.then_inc(s["idx_ok"], 1)
                    else:
                        link(ins)
                link(dve.tensor_reduce(ohsum[:, :], OHB[:, :, :].rearrange("p t e -> p e t"), AX_X, ALU.add))
                link(tt(OHacc[:, :], OHacc[:, :], ohsum[:, :], ALU.add))
                dve.wait_ge(s["idx_ok"], quad + 1)
                assert c[0] == R3N[l], c

            def body(l, b, k, q):
                n, p, at = NB * l + b, k % 2, (l, b, k, q)
                if here(b):
                    max_sub(n, 1)
                if here(b + 1):
                    nk = (k + 1) % 4
                    dve.wait_ge(s["rstd1_ok"], n + 2)
                    ts(xn[:, 1 - p, :], X[:, bass.ds(b + 1, 1), :].rearrange("p a d -> p (a d)"), mv1[:, nk, 0:1], rstd1[:, nk:nk + 1],
                       ALU.subtract, ALU.mult).then_inc(s["xn_ok"], 1)
                if here(b):
                    sums(n, p, 0)
                if here(b - 1):
                    dve.wait_ge(s["b_full"], b_turn(*at, "pv"))
                    dve.wait_ge(s["a_read"], a_turn(*at, "rT"))
                    tt(OT[:, 1 - p, :], B[:, 0:P], RT[:, 1 - p, :], ALU.mult).then_inc(s["b_read"], 1)
                    dve.sem_inc(s["pv_done"], 1)
                if here(b + 1):
                    wait(dve, s["s_ok"], 2 * n)
                    dve.wait_ge(s["b_full"], b_turn(*at, "cT"))
                    dve.sem_inc(s["cT_ok"], 1)
                    if l:
                        cp(cT[:, 1 - p, :], B[:, 128:128 + NK]).then_inc(s["b_read"], 1)
                        dve.wait_ge(s["b_full"], b_turn(*at, "kv"))
                    keys = B[:, 256:256 + NK] if l else B[:, 128:128 + NK]
                    if l:
                        for g in range(G):
                            ins = cp(VP[:, 1 - p, g, :].rearrange("k (j c) -> k j c", c=40)[:, :, 0:DH],
                                     B[0:NK, 384 + 32 * g:384 + 32 * g + 32].rearrange("k (j c) -> k j c", c=DH))
                        ins.then_inc(s["vp_ok"], 1)
                    tt(KB[:, 1 - p, :].rearrange("p (j k) -> p j k", j=J), keys[:, None, :].to_broadcast([P, J, NK]),
                       own[:, :, None].to_broadcast([P, J, NK]), ALU.mult).then_inc(s["b_read"], 1)
                    max_sub(n + 1, 0)
                if here(b):
                    sums(n, p, 1)
                    dve.wait_ge(s["sum_ok"], 2 * n + 2)
                    dve.reciprocal(R[:, p, :].rearrange("p (h d) -> p h d", d=DH),
                                   SUM[:, p, :, None].to_broadcast([P, NH, DH])).then_inc(s["recip_ok"], 1)
                if here(b - 1):
                    dve.wait_ge(s["b_full"], b_turn(*at, "proj"))
                    xb = X[:, bass.ds(b - 1, 1), :].rearrange("p a d -> p (a d)")
                    tt(xb, B[:, 256:384], xb, ALU.add).then_inc(s["b_read"], 1)
                    dve.wait_ge(s["b_read"], b_turn(*at, "proj"))
                    stats(xb, n - 1, 1 - p, (k - 1) % 4, st2, mv2, "st2_ok", "mv2_ok")
                if here(b - 3):
                    dve.wait_ge(s["b_full"], b_turn(*at, "lg"))
                    cp(LG[:, (k - 3) % 4, :], B[:, 384:384 + E]).then_inc(s["b_read"], 1)
                if here(b - 2):
                    dve.wait_ge(s["rstd2_ok"], n - 1)
                    kk = (k - 2) % 4
                    xb = X[:, bass.ds(b - 2, 1), :].rearrange("p a d -> p (a d)")
                    ts(XN2[:, bass.ds(b - 2, 1), :].rearrange("p a d -> p (a d)"), xb, mv2[:, kk, 0:1], rstd2[:, kk:kk + 1],
                       ALU.subtract, ALU.mult).then_inc(s["xn2_ok"], 1)
                    ts(xg[:, p, :], xb, mv2[:, kk, 0:1], rstd2[:, kk:kk + 1],
                       ALU.subtract, ALU.mult).then_inc(s["xg_ok"], 1)
                if here(b + 2):
                    kk = (k + 2) % 4
                    if l:
                        combine(0, b + 2, kk, q + (k + 2) // 4)
                        dve.wait_ge(s["combined"], b + 3)
                    else:
                        dve.wait_ge(x_ld[0], 16)
                        if not isinstance(b, int) or b + 2 >= 4:
                            dve.wait_ge(x_ld[1], 16)
                    stats(X[:, bass.ds(b + 2, 1), :].rearrange("p a d -> p (a d)"), n + 2, p, kk, st1, mv1, "st1_ok", "mv1_ok")
                if k == 2 and here(b - 6):
                    dve.wait_ge(s["b_read"], b_turn(*at, "lg"))
                    route1(l, 4 * l + q - 1)
                if k == 3 and here(b - 7):
                    dve.wait_ge(s["consts_ok"], 1)
                    route2(l, 4 * l + q - 1, (q - 1) * 4)
                    route3(l, 4 * l + q - 1, (q - 1) * 4, b_turn(*at, "prefix"))

            def tables(l):
                link, c = chain("tab", l * TABN[0])
                nt = TILES[l]
                dve.wait_ge(s["b_full"], counts_turn(l))
                cp(cnt[:, :], B[:, 0:E]).then_inc(s["b_read"], 1)
                dve.wait_ge(s["b_read"], counts_turn(l))
                link(ts(cnti[:, :], cnt[:, :], float(P - 1), None, ALU.add))
                link(ts(nti[:, :], cnti[:, :], 7, None, ALU.arith_shift_right))
                link(cp(ntf[:, :], nti[:, :]))
                link(cp(cum[:, 0, 4:], nti[:, :]))
                for i, d in enumerate((1, 2, 4)):
                    link(tt(cum[:, i + 1, 4:], cum[:, i, 4:], cum[:, i, 4 - d:4 + E - d], ALU.add))
                total = cum[0:1, 3, 3 + E:4 + E]
                shape = [1, nt, E - 1]
                link(tt(ge[:, 0:nt, :], tile_no[:, 0:nt, :], cum[0:1, 3, None, 4:3 + E].to_broadcast(shape), ALU.is_ge))
                link(dve.tensor_reduce(tef[:, 0:nt], ge[:, 0:nt, :], AX_X, ALU.add))
                link(tt(gen[:, 0:nt, :], ge[:, 0:nt, :], ntf[0:1, None, 0:E - 1].to_broadcast(shape), ALU.mult))
                link(dve.tensor_reduce(startf[:, 0:nt], gen[:, 0:nt, :], AX_X, ALU.add))
                link(ts(validf[:, 0:nt], tile_no[:, 0:nt, 0], total, None, ALU.is_lt))
                link(tt(offf[:, 0:nt], tile_no[:, 0:nt, 0], startf[:, 0:nt], ALU.subtract))
                link(dve.scalar_tensor_tensor(out=offf[:, 0:nt], in0=offf[:, 0:nt], scalar=float(P), in1=validf[:, 0:nt],
                                              op0=ALU.mult, op1=ALU.mult))
                link(dve.scalar_tensor_tensor(out=rowf[:, 0:nt], in0=tef[:, 0:nt], scalar=float(REGION), in1=offf[:, 0:nt],
                                              op0=ALU.mult, op1=ALU.add))
                link(cp(ROW[l][:, :], rowf[:, 0:nt]))
                link(cp(TE[l][:, :], tef[:, 0:nt]))
                link(tt(fillf[:, :], cnt[0:1, :], region0[0:1, 0, :], ALU.add))
                cp(FILL[l][:, :], fillf[:, :]).then_inc(s["tables_ok"], 1)
                link(dve.memset(OHacc[:, :], 0.0))
                link(tt(shift[:, :], cum[:, 3, 4:], ntf[:, :], ALU.subtract))
                link(dve.scalar_tensor_tensor(out=shift[:, :], in0=shift[:, :], scalar=float(P), in1=region0[:, 0, :],
                                              op0=ALU.mult, op1=ALU.subtract))
                for k in range(TOPK[l]):
                    link(tt(moved[:, :, :], OH[:, k, :, :], shift[:, None, :].to_broadcast([P, NB, E]), ALU.mult))
                    link(dve.tensor_reduce(movedr[:, :], moved[:, :, :], AX_X, ALU.add))
                    link(tt(movedr[:, :], movedr[:, :], POSF[:, k, :], ALU.add))
                    link(cp(IDXG[l][:, k, :], movedr[:, :]))
                dve.sem_inc(s["idxg_ok"], 1)
                assert c[0] == TABN[l], c

            for l in range(2):
                over_batches(dve, l, body)
                tables(l)

                def tile(l, r, k, j):
                    m = T0[l] + r
                    if tile_here(l, r - 1):
                        kk = (k - 1) % 4
                        dve.wait_ge(s["y_ok"], m)
                        wait(dve, y_st[kk], (j + (k - 1) // 4 + SLOT0[l][kk]) * 16)
                        cp(Y[:, kk, :], PTp[:, kk % 2, 0:D]).then_inc(s["y_used"], 1)
                    if tile_here(l, r):
                        dve.wait_ge(s["hT_ok"], m + 1)
                        wait(dve, s["y_ok"], m - 1)
                        cp(HT[:, k % 2, 0:FF[l]], S[:, 2 + k % 2, 0:FF[l]]).then_inc(s["hT_used"], 1)

                over_tiles(dve, l, tile, 2, 1)
            for b in range(NB):
                combine(1, b, b % 4, b // 4)


_INS = ['x', 'ctx_1024', 'mask_Bx1xSxS2_ik1', 'mask_1x1xSxS2_if1', 'L0_xattn_W_fc', 'L0_xattn_b_fc', 'L0_ffn_gate',
        'L0_ffn_W1', 'L0_ffn_b1', 'L0_ffn_W2', 'L0_ffn_b2', 'L1_xattn_W_Q', 'L1_xattn_W_K', 'L1_xattn_W_V',
        'L1_xattn_W_T', 'L1_ffn_gate_w', 'L1_ffn_w1', 'L1_ffn_b1', 'L1_ffn_w2', 'L1_ffn_b2']


def kernel(**inputs):
    import numpy as _np
    import concourse.bacc as _bacc
    from concourse import mybir as _mybir
    from concourse.bass_utils import run_bass_kernel_spmd as _run

    nc = _bacc.Bacc("TRN2", target_bir_lowering=False, num_devices=1)
    arrays, args = {}, []
    for name in _INS:
        a = _np.ascontiguousarray(inputs[name])
        arrays[f"in_{name}_dram"] = a
        args.append(nc.dram_tensor(f"in_{name}_dram", a.shape, _mybir.dt.from_np(a.dtype), kind="ExternalInput").ap())
    args.append(nc.dram_tensor("out_dram", (16, 128, 128), _mybir.dt.float32, kind="ExternalOutput").ap())
    build(nc, *args)
    r = _run(nc, [arrays], core_ids=[0])
    return r.results[0]["out_dram"]
```

```python
from contextlib import ExitStack

import concourse.bass as bass
from concourse import mybir

F32 = mybir.dt.float32
BF16 = mybir.dt.bfloat16
I32 = mybir.dt.int32
U32 = mybir.dt.uint32
ALU = mybir.AluOpType
ACT = mybir.ActivationFunctionType
AX_X = mybir.AxisListType.X

P = 128
NB = 16
D = 128
NH = 16
DH = D // NH
NK = 77
G = 4
J = NH // G
GK = J * NK
E = 8
QT = 4
REGION = NB * P + P
SPARE = E * REGION
NEG = -1e20
EPS = 1e-5
FF = (256, 512)
TOPK = (2, 1)
TILES = tuple(NB * k + E - 1 for k in TOPK)
EBITS = E.bit_length() - 1
WORD = 6
NW = tuple(t // 4 + 2 for t in TILES)
SCALE = (float(D) ** -0.5, float(DH) ** -0.5)


def wait(eng, sem, value):
    if not isinstance(value, int) or value > 0:
        eng.wait_ge(sem, value)


def here(b):
    return not isinstance(b, int) or 0 <= b < NB


def build(nc, x, ctx_in, mask0, mask1, wfc, bfc, gate0, w1_0, b1_0, w2_0, b2_0,
          wq, wk, wv, wt, gate1, w1_1, b1_1, w2_1, b2_1, out):
    xs = nc.dram_tensor("sorted_rows", (SPARE + P, D), F32).ap()
    ys = nc.dram_tensor("sorted_outputs", (max(TILES) * P, D), F32).ap()
    with ExitStack() as stack:
        def sb(name, shape, dt=F32):
            return stack.enter_context(nc.sbuf_tensor(name, shape, dt))

        def pb(name, shape, dt=F32):
            return stack.enter_context(nc.psum_tensor(name, shape, dt))

        def sem(name):
            return stack.enter_context(nc.semaphore(name))

        X = sb("X", [P, NB, D])
        W1 = [sb(f"W1_{l}", [P, E * FF[l]]) for l in range(2)]
        W2 = [sb(f"W2_{l}", [P, E * FF[l]]) for l in range(2)]
        b1row = [sb(f"b1row{l}", [E, FF[l]]) for l in range(2)]
        b2row = [sb(f"b2row{l}", [E, D]) for l in range(2)]
        b1rem = [sb(f"b1rem{l}", [E, 2, FF[l]]) for l in range(2)]
        b2rem = [sb(f"b2rem{l}", [E, 2, D]) for l in range(2)]
        b1part = [sb(f"b1part{l}", [E, 3, FF[l]], BF16) for l in range(2)]
        b2part = [sb(f"b2part{l}", [E, 3, D], BF16) for l in range(2)]
        b1s = [sb(f"b1s{l}", [3, E * FF[l]], BF16) for l in range(2)]
        b2s = [sb(f"b2s{l}", [3, E * D], BF16) for l in range(2)]
        gate = [sb(f"gate{l}", [P, E]) for l in range(2)]
        wfc_sb = sb("wfc_sb", [P, D])
        wfcT = sb("wfcT", [P, D])
        wq_sb, wk_sb, wv_sb, wt_sb = (sb(n, [P, D]) for n in ("wq_sb", "wk_sb", "wv_sb", "wt_sb"))
        bfc_sb = sb("bfc_sb", [1, D])
        ident = sb("ident", [P, P])
        identb = sb("identb", [P, P], BF16)
        ones_f = sb("ones_f", [P, P])
        onesb = sb("onesb", [P, P], BF16)
        before = sb("before", [P, P], BF16)
        own_a = sb("own_a", [P, J])
        own = sb("own", [P, J])
        zeros = sb("zeros", [P, D])
        minus_half = sb("minus_half", [P, 1])
        region0 = sb("region0", [P, QT, E])
        revf = sb("revf", [P, QT, E])
        iot = sb("iot", [P, QT, E], I32)
        tile_no_i = sb("tile_no_i", [1, max(TILES), E - 1], I32)
        tile_no = sb("tile_no", [1, max(TILES), E - 1])
        mask0_sb = sb("mask0_sb", [P, NB, NK], I32)
        mask1_sb = sb("mask1_sb", [P, NK], I32)
        ctx = sb("ctx", [NK, QT, D])
        bias = sb("bias", [P, 2, NK], BF16)
        bias1 = sb("bias1", [P, NK], BF16)
        st1 = sb("st1", [P, 2, 6])
        mv1 = sb("mv1", [P, 4, 2])
        ve1 = sb("ve1", [P, 4])
        rstd1 = sb("rstd1", [P, 4])
        st2 = sb("st2", [P, 2, 6])
        mv2 = sb("mv2", [P, 4, 2])
        ve2 = sb("ve2", [P, 4])
        rstd2 = sb("rstd2", [P, 4])
        xn = sb("xn", [P, 2, D])
        xT = sb("xT", [P, 2, P])
        qTs = sb("qTs", [P, 2, P])
        cT = sb("cT", [P, 2, NK])
        kTs = sb("kTs", [P, 2, NK])
        Vs = sb("Vs", [NK, 2, D])
        KB = sb("KB", [P, 2, GK])
        OV = sb("OV", [NK, 160])
        VP = sb("VP", [NK, 2, G, 160])
        M = sb("M", [P, 2, 2 * J])
        SB = sb("SB", [P, 2, 2 * GK])
        PR = sb("PR", [P, 2, 2 * GK])
        PT = sb("PT", [NK, 2, NH * P])
        total = sb("total", [P, P])
        OT = sb("OT", [P, 2, P])
        XN2 = sb("XN2", [P, NB, D])
        xg = sb("xg", [P, 2, D])
        xgT = sb("xgT", [P, 2, P])
        LG = sb("LG", [P, QT, E])
        rmax = sb("rmax", [P, QT])
        rsub = sb("rsub", [P, QT, E])
        rexp = sb("rexp", [P, QT, E])
        rsum = sb("rsum", [P, QT])
        rrec = sb("rrec", [P, QT])
        prob = sb("prob", [P, QT, E])
        val = sb("val", [P, 2, QT])
        eq = sb("eq", [P, QT, E])
        rank = sb("rank", [P, QT, E])
        first = sb("first", [P, QT])
        OH = sb("OH", [P, 2, NB, E])
        prob2 = sb("prob2", [P, QT, E])
        gden = sb("gden", [P, QT])
        OHB = sb("OHB", [P, QT, E], BF16)
        ohsum = sb("ohsum", [P, E])
        OHacc = sb("OHacc", [P, E], BF16)
        pos = sb("pos", [P, QT, E])
        posk = sb("posk", [P, QT, E])
        POSF = sb("POSF", [P, 2, NB])
        IDX = [sb(f"IDX{l}", [P, 2, NB], I32) for l in range(2)]
        IDXG = [sb(f"IDXG{l}", [P, 2, NB], I32) for l in range(2)]
        GV = [sb(f"GV{l}", [P, 2, NB]) for l in range(2)]
        cnt = sb("cnt", [P, E])
        cnti = sb("cnti", [P, E], I32)
        nti = sb("nti", [P, E], I32)
        ntf = sb("ntf", [P, E])
        cum = sb("cum", [P, 4, 4 + E])
        ge = sb("ge", [1, max(TILES), E - 1])
        gen = sb("gen", [1, max(TILES), E - 1])
        tef = sb("tef", [1, 4 * max(NW) + WORD - 1])
        packf = sb("packf", [1, max(NW)])
        startf = sb("startf", [1, max(TILES)])
        validf = sb("validf", [1, max(TILES)])
        offf = sb("offf", [1, max(TILES)])
        rowf = sb("rowf", [1, max(TILES)])
        shift = sb("shift", [P, E])
        moved = sb("moved", [P, NB, E])
        movedr = sb("movedr", [P, NB])
        fillf = sb("fillf", [1, E])
        TE = [sb(f"TE{l}", [1, NW[l]], I32) for l in range(2)]
        ROW = [sb(f"ROW{l}", [1, TILES[l]], I32) for l in range(2)]
        FILL = [sb(f"FILL{l}", [1, E], I32) for l in range(2)]
        xt = sb("xt", [P, 4, D])
        xtT = sb("xtT", [P, 2, P])
        H = sb("H", [P, 2, max(FF)])
        HT = sb("HT", [P, 2, max(FF)])
        Y = sb("Y", [P, 4, D])
        YG = sb("YG", [P, 4, 2, D])

        S = pb("S", [P, G, 512])
        PTp = pb("PTp", [P, 2, 512])
        A = pb("A", [P, 512])
        B = pb("B", [P, 512])

        names = ("w_ok proj_ld wfc_ld mask_ld bias_ld bias_split bias_parts pool_chain ident_ok consts_ok "
                 "a_full a_read b_full b_read bias1_ok bias_ok vp_ok "
                 "combined comb_part st1_ok mv1_ok ve1_ok rstd1_ok xn_ok "
                 "s_ok m_ok sub_ok exp_ok pt_ok pt_used kb_ok total_ok pv_done "
                 "st2_ok mv2_ok ve2_ok rstd2_ok xn2_ok xg_ok r1 rexp_ok r2 r3  ohb_ok idx_ok tab tables_ok idxg_ok "
                 "scattered filled xtT_ok xtT_used h_ok h_used hT_ok hT_used y_ok y_used stored held").split()
        s = {n: sem(n) for n in names}
        ctx_ld = [sem(f"ctx_ld{i}") for i in range(4)]
        x_ld = [sem(f"x_ld{i}") for i in range(2)]
        xt_ld = [sem(f"xt_ld{i}") for i in range(4)]
        y_st = [sem(f"y_st{i}") for i in range(4)]
        gath = [sem(f"gath{i}") for i in range(4)]
        block = stack.enter_context(nc.Block())

        R1N, R2N, R3N, TABN = 2, (18, 9), (7, 4), (35, 31)
        W_ALL = 16 * 2 * (1 + E)
        FIRST, LAST = -3, NB + 4

        def over_batches(eng, l, body):
            for b in range(FIRST, 4):
                body(l, b, b % 4, b // 4)
            with eng.Fori(1, 3) as i:
                for k in range(4):
                    body(l, i * 4 + k, k, i)
            for b in range(NB - 4, LAST):
                body(l, b, b % 4, b // 4)

        def over_tiles(eng, l, body, lead, lag):
            n = TILES[l]
            top = (n - lead) // 4 * 4
            for r in range(-lead, 4):
                body(l, r, r % 4, r // 4)
            with eng.Fori(1, top // 4) as i:
                for k in range(4):
                    body(l, i * 4 + k, k, i)
            for r in range(top, n + lag):
                body(l, r, r % 4, r // 4)

        def tile_here(l, r):
            return not isinstance(r, int) or 0 <= r < TILES[l]

        T0 = (0, TILES[0])
        SLOT0 = ([0] * 4, [len(range(k, TILES[0], 4)) for k in range(4)])

        def a_uses(l, b):
            return ((["xc"] if here(b + 2) else []) + (["qkv"] if l and (here(b + 2) or here(b + 1)) else [])
                    + (["gl"] if here(b - 2) or here(b - 3) else []))

        def b_uses(l, b):
            return ((["pv", "proj"] if here(b - 1) else [])
                    + (["prefix"] if b % 4 == 3 and 0 <= b - 7 < NB else []))

        def turn(uses, l, b, k, q, stage):
            def at(b):
                n = 1 if uses is a_uses else 0
                if l:
                    n += sum(len(uses(0, c)) for c in range(FIRST, LAST)) + (uses is b_uses)
                n += sum(len(uses(l, c)) for c in range(FIRST, b))
                return n + uses(l, b).index(stage) + 1
            if isinstance(b, int):
                return at(b)
            c = at(4 + k)
            d = at(8 + k) - c
            return q * d + (c - d)

        def a_turn(*x):
            return turn(a_uses, *x)

        def b_turn(*x):
            return turn(b_uses, *x)

        def counts_turn(l):
            return sum(len(b_uses(i, c)) + 0 for i in range(l + 1) for c in range(FIRST, LAST)) + l + 1

        @block.sync
        def _(sp):
            xv = x.rearrange("b p d -> p b d")
            sp.dma_start(X[:, 0:4, :], xv[:, 0:4, :]).then_inc(x_ld[0], 16)

            def load_ctx(l, b, k):
                n = NB * l + b
                wait(sp, s["kb_ok"], n - 3)
                wait(sp, s["vp_ok"], n - 3)
                sp.dma_start(ctx[:, k, :], ctx_in[b, :, :]).then_inc(ctx_ld[k], 16)

            for b in range(4):
                load_ctx(0, b, b)
            sp.dma_start(wfc_sb[:, :], wfc).then_inc(s["wfc_ld"], 16)
            sp.dma_start(bfc_sb[:, :], bfc.rearrange("(a d) -> a d", a=1)).then_inc(s["wfc_ld"], 16)
            sp.dma_start(mask0_sb[:, :, :], mask0.rearrange("b o q k -> q (b o) k")).then_inc(s["mask_ld"], 16)
            sp.dma_start(mask1_sb[:, :], mask1.rearrange("a o q k -> q (a o k)")).then_inc(s["mask_ld"], 16)
            sp.dma_start(X[:, 4:NB, :], xv[:, 4:NB, :]).then_inc(x_ld[1], 16)
            for dst, src in ((gate[0], gate0), (gate[1], gate1), (wq_sb, wq), (wk_sb, wk), (wv_sb, wv), (wt_sb, wt)):
                sp.dma_start(dst[:, :], src).then_inc(s["proj_ld"], 16)
            for l, (b1, b2) in enumerate(((b1_0, b2_0), (b1_1, b2_1))):
                sp.dma_start(b1row[l][:, :], b1).then_inc(s["bias_ld"], 16)
                sp.dma_start(b2row[l][:, :], b2).then_inc(s["bias_ld"], 16)
            for l, (w1, w2) in enumerate(((w1_0, w2_0), (w1_1, w2_1))):
                sp.dma_start(W1[l][:, :].rearrange("p (e f) -> p e f", e=E),
                             w1.rearrange("e d f -> d e f")).then_inc(s["w_ok"], 16)
                for e in range(E):
                    sp.dma_start(W2[l][:, e * FF[l]:(e + 1) * FF[l]].rearrange("p (c d) -> p c d", d=D),
                                 w2[e, :, :].rearrange("(c p) d -> p c d", p=P)).then_inc(s["w_ok"], 16)
            for l in range(2):
                if l:
                    for b in range(4):
                        load_ctx(l, b, b)
                with sp.Fori(1, 4) as i:
                    for k in range(4):
                        load_ctx(l, i * 4 + k, k)
                if l == 0:
                    sp.wait_ge(s["bias_split"], 1)
                    for i in range(2):
                        for c in range(3):
                            sp.dma_start(b1s[i][c:c + 1, :].rearrange("p (e f) -> p e f", e=E),
                                         b1part[i][:, c, :]).then_inc(s["bias_parts"], 16)
                            sp.dma_start(b2s[i][c:c + 1, :].rearrange("p (e f) -> p e f", e=E),
                                         b2part[i][:, c, :]).then_inc(s["bias_parts"], 16)
                sp.wait_ge(s["tables_ok"], l + 1)
                sp.wait_ge(s["consts_ok"], 1)
                for e in range(E):
                    row = sp.value_load(FILL[l][0:1, e:e + 1], min_val=0, max_val=SPARE)
                    sp.dma_start(xs[bass.ds(row, P), :], zeros[:, :]).then_inc(s["filled"], 16)
                sp.wait_ge(s["filled"], 16 * E * (l + 1))
                sp.wait_ge(s["scattered"], 16 * NB * (TOPK[0] + l * TOPK[1]))

                def tile(l, r, k, j):
                    m = T0[l] + r
                    if tile_here(l, r + 4):
                        wait(sp, s["xtT_ok"], m + 1)
                        row = sp.value_load(ROW[l][0:1, bass.ds(r + 4, 1)], min_val=0, max_val=SPARE)
                        sp.dma_start(xt[:, k, :], xs[bass.ds(row, P), :]).then_inc(xt_ld[k], 16)
                    if tile_here(l, r - 2):
                        sp.wait_ge(s["y_used"], m - 1)
                        sp.dma_start(ys[bass.ds((r - 2) * P, P), :], Y[:, (k - 2) % 4, :]).then_inc(y_st[(k - 2) % 4], 16)

                over_tiles(sp, l, tile, 4, 2)
            with sp.Fori(0, NB) as b:
                sp.wait_ge(s["combined"], b + (NB + 1))
                sp.dma_start(out[b, :, :], X[:, b, :]).then_inc(s["stored"], 16)
            sp.wait_ge(s["stored"], 16 * NB)

        @block.gpsimd
        def _(pool):
            count = [0]

            def link(ins):
                count[0] += 1
                ins.then_inc(s["pool_chain"], 1)
                pool.wait_ge(s["pool_chain"], count[0])

            link(pool.memset(ones_f[:, :], 1.0))
            link(pool.memset(minus_half[:, :], -0.5))
            pool.affine_select(out=ident[:, :], in_=ones_f[:, :], compare_op=ALU.is_equal, fill=0.0, base=0,
                               pattern=[[-1, P]], channel_multiplier=1).then_inc(s["ident_ok"], 1)
            pool.wait_ge(s["ident_ok"], 1)
            link(pool.tensor_copy(identb[:, :], ident[:, :]))
            for g in range(G):
                rows = slice(32 * g, 32 * g + 32)
                link(pool.affine_select(out=own_a[rows, :], in_=ones_f[rows, 0:J], compare_op=ALU.is_ge, fill=0.0,
                                        base=0, pattern=[[-DH, J]], channel_multiplier=1))
                link(pool.affine_select(out=own[rows, :], in_=own_a[rows, :], compare_op=ALU.is_ge, fill=0.0,
                                        base=DH - 1, pattern=[[DH, J]], channel_multiplier=-1))
            pool.wait_ge(s["mask_ld"], 32)
            pool.tensor_scalar(bias1[:, :], mask1_sb[:, :], 0.0, NEG, ALU.is_equal, ALU.mult).then_inc(s["bias1_ok"], 1)
            link(pool.memset(VP[:, :, :, :], 0.0))
            link(pool.memset(OV[:, :], 0.0))
            link(pool.memset(OV[:, :].rearrange("k (j c) -> k j c", c=40)[:, :, 0:DH], 1.0))

            def constants():
                link(pool.memset(zeros[:, :], 0.0))
                link(pool.memset(OHacc[:, :], 0.0))
                link(pool.memset(cum[:, :, :], 0.0))
                link(pool.memset(tef[:, :], 0.0))
                link(pool.tensor_copy(onesb[:, :], ones_f[:, :]))
                link(pool.affine_select(out=before[:, :], in_=onesb[:, :], compare_op=ALU.is_gt, fill=0.0, base=0,
                                        pattern=[[1, P]], channel_multiplier=-1))
                link(pool.iota(iot[:, :, :], pattern=[[0, QT], [REGION, E]], base=0, channel_multiplier=0))
                link(pool.tensor_copy(region0[:, :, :], iot[:, :, :]))
                link(pool.iota(iot[:, :, :], pattern=[[0, QT], [-1, E]], base=E, channel_multiplier=0))
                link(pool.tensor_copy(revf[:, :, :], iot[:, :, :]))
                link(pool.iota(tile_no_i[:, :, :], pattern=[[1, max(TILES)], [0, E - 1]], base=0, channel_multiplier=0))
                pool.tensor_copy(tile_no[:, :, :], tile_no_i[:, :, :]).then_inc(s["consts_ok"], 1)

            def split_biases(l):
                pool.wait_ge(s["bias_ld"], 64)
                for row, rem, part in ((b1row[l], b1rem[l], b1part[l]), (b2row[l], b2rem[l], b2part[l])):
                    link(pool.tensor_copy(part[:, 0, :], row[:, :]))
                    link(pool.tensor_tensor(rem[:, 0, :], row[:, :], part[:, 0, :], ALU.subtract))
                    link(pool.tensor_copy(part[:, 1, :], rem[:, 0, :]))
                    link(pool.tensor_tensor(rem[:, 1, :], rem[:, 0, :], part[:, 1, :], ALU.subtract))
                    link(pool.tensor_copy(part[:, 2, :], rem[:, 1, :]))
                if l:
                    pool.sem_inc(s["bias_split"], 1)

            def rstd(n, k, mv, ve, rs, mv_ok, ve_ok, rs_ok):
                pool.wait_ge(s[mv_ok], n + 1)
                pool.tensor_scalar(ve[:, k:k + 1], mv[:, k, 1:2], EPS, None, ALU.add).then_inc(s[ve_ok], 1)
                pool.wait_ge(s[ve_ok], n + 1)
                pool.tensor_tensor(rs[:, k:k + 1], ve[:, k:k + 1], minus_half[:, :], ALU.pow).then_inc(s[rs_ok], 1)

            def body(l, b):
                n, p = NB * l + b, b % 2
                if l == 0 and here(b + 2):
                    wait(pool, s["s_ok"], 2 * n + 2)
                    pool.tensor_scalar(bias[:, p, :], mask0_sb[:, b + 2, :], 0.0, NEG, ALU.is_equal,
                                       ALU.mult).then_inc(s["bias_ok"], 1)
                if here(b):
                    if l:
                        pool.wait_ge(s["a_read"], a_turn(l, b - 1, (b - 1) % 4, (b - 1) // 4, "qkv"))
                    else:
                        pool.wait_ge(ctx_ld[b % 4], 16 * (b // 4 + 1))
                    wait(pool, s["pv_done"], n - 1)
                    values = Vs[:, p, :] if l else ctx[:, b % 4, :]
                    for g in range(G):
                        v = pool.tensor_copy(VP[:, p, g, :].rearrange("k (j c) -> k j c", c=40)[:, :, 0:DH],
                                             values[:, 32 * g:32 * g + 32].rearrange("k (j c) -> k j c", c=DH))
                    v.then_inc(s["vp_ok"], 1)
                if here(b - 2):
                    t, k = b - 2, (b - 2) % 4
                    pool.wait_ge(s["rstd2_ok"], n - 1)
                    pool.tensor_scalar(XN2[:, t, :], X[:, t, :], mv2[:, k, 0:1], rstd2[:, k:k + 1],
                                       ALU.subtract, ALU.mult).then_inc(s["xn2_ok"], 1)
                if here(b - 8):
                    t = b - 8
                    pool.wait_ge(s["idx_ok"], 4 * l + t // 4 + 1)
                    pool.wait_ge(s["xn2_ok"], NB * l + t + 1)
                    for k in range(TOPK[l]):
                        pool.indirect_dma_start(
                            out=xs, out_offset=bass.IndirectOffsetOnAxis(ap=IDX[l][:, k, t:t + 1].bitcast(U32), axis=0),
                            in_=XN2[:, t, :], in_offset=None).then_inc(s["scattered"], 16)
                if here(b - 1):
                    wait(pool, s["xg_ok"], n - 4)
                    rstd(n - 1, (b - 1) % 4, mv2, ve2, rstd2, "mv2_ok", "ve2_ok", "rstd2_ok")
                if here(b + 3):
                    wait(pool, s["xn_ok"], n)
                    rstd(n + 3, (b + 3) % 4, mv1, ve1, rstd1, "mv1_ok", "ve1_ok", "rstd1_ok")

            def gather(l, t):
                wait(pool, s["combined"], NB * l + t - 3)
                for k in range(TOPK[l]):
                    pool.indirect_dma_start(
                        out=YG[:, t % 4, k, :], out_offset=None, in_=ys,
                        in_offset=bass.IndirectOffsetOnAxis(ap=IDXG[l][:, k, t:t + 1].bitcast(U32), axis=0),
                    ).then_inc(gath[t % 4], 16)

            for l in range(2):
                for b in range(FIRST, NB + 8):
                    if l and b == FIRST:
                        for t in range(4):
                            gather(0, t)
                    body(l, b)
                    if l == 0 and b == 0:
                        constants()
                    if l == 0 and b in (3, 4):
                        split_biases(b - 3)
                    if l and 4 <= b + 7 < NB:
                        gather(0, b + 7)
                pool.wait_ge(s["idxg_ok"], l + 1)
                for k in range(4):
                    pool.wait_ge(y_st[k], 16 * sum(len(range(k, TILES[i], 4)) for i in range(l + 1)))
            for t in range(NB):
                gather(1, t)

        @block.scalar
        def _(act):
            def exps(l, n, h):
                wait(act, s["sub_ok"], 2 * n + h + 1)
                wait(act, s["pt_ok"], 4 * n + 2 * h - 2)
                act.activation(PR[:, h, :], SB[:, h, :], ACT.Exp, scale=SCALE[l]).then_inc(s["exp_ok"], 1)

            def probs_out(n, p, h):
                wait(act, s["pv_done"], n - 1)
                for q in range(2):
                    wait(act, s["pt_ok"], 4 * n + 2 * h + q + 1)
                    at = (2 * h + q) * J * P
                    act.copy(PT[:, p, at:at + J * P], PTp[0:NK, q, :]).then_inc(s["pt_used"], 1)

            def body(l, b, k, q):
                n, p, at = NB * l + b, k % 2, (l, b, k, q)
                if here(b):
                    exps(l, n, 1)
                    probs_out(n, p, 0)
                if here(b + 2):
                    act.wait_ge(s["a_full"], a_turn(*at, "xc"))
                    wait(act, s["s_ok"], 2 * n + 2)
                    act.copy(xT[:, p, :], A[:, 0:P])
                    act.copy(cT[:, p, :], A[:, P:P + NK]).then_inc(s["a_read"], 1)
                if l and (here(b + 2) or here(b + 1)):
                    act.wait_ge(s["a_full"], a_turn(*at, "qkv"))
                    if here(b + 2):
                        act.copy(qTs[:, p, :], A[:, 0:P])
                        ins = act.copy(kTs[:, p, :], A[:, P:P + NK])
                    if here(b + 1):
                        wait(act, s["vp_ok"], n)
                        ins = act.copy(Vs[:, 1 - p, :], A[0:NK, 2 * P:3 * P])
                    ins.then_inc(s["a_read"], 1)
                if here(b):
                    probs_out(n, p, 1)
                if here(b + 1):
                    exps(l, n + 1, 0)
                if here(b - 2) or here(b - 3):
                    act.wait_ge(s["a_full"], a_turn(*at, "gl"))
                    if here(b - 2):
                        ins = act.copy(xgT[:, p, :], A[:, 0:P])
                    if here(b - 3):
                        ins = act.copy(LG[:, (k - 3) % 4, :], A[:, P:P + E])
                    ins.then_inc(s["a_read"], 1)
                if k == 2 and here(b - 6):
                    act.wait_ge(s["r1"], 2 * (4 * l + q - 1) + 2)
                    act.activation(rexp[:, :, :], rsub[:, :, :], ACT.Exp).then_inc(s["rexp_ok"], 1)

            act.wait_ge(s["a_full"], 1)
            act.copy(wfcT[:, :], A[:, 0:P]).then_inc(s["a_read"], 1)
            for l in range(2):
                over_batches(act, l, body)

                def tile(l, r, k, j):
                    m = T0[l] + r
                    if tile_here(l, r + 1):
                        act.wait_ge(s["h_ok"], m + 2)
                        wait(act, s["hT_ok"], m)
                        act.activation(H[:, (k + 1) % 2, 0:FF[l]], S[:, (k + 1) % 2, 0:FF[l]],
                                       ACT.Gelu if l else ACT.Relu).then_inc(s["h_used"], 1)
                    if tile_here(l, r + 2):
                        act.wait_ge(s["xtT_ok"], m + 3)
                        wait(act, s["h_ok"], m + 1)
                        act.copy(xtT[:, k % 2, :], A[:, 0:P]).then_inc(s["xtT_used"], 1)

                over_tiles(act, l, tile, 2, 0)

        @block.tensor
        def _(pe):
            mm = pe.matmul

            def scores(l, b, k, q, h):
                n, p = NB * l + b, k % 2
                pe.wait_ge(s["kb_ok"], n + 1)
                if l:
                    pe.wait_ge(s["bias1_ok"], 1)
                else:
                    pe.wait_ge(s["bias_ok"], n + 1)
                wait(pe, s["sub_ok"], 2 * n + h - 1)
                queries = qTs if l else xT
                mask = bias1[:, :] if l else bias[:, p, :]
                for g in (2 * h, 2 * h + 1):
                    rows = slice(32 * g, 32 * g + 32)
                    mm(S[:, g, 0:GK], queries[rows, p, :], KB[rows, p, :], start=True, stop=False)
                for g in (2 * h, 2 * h + 1):
                    last = mm(S[:, g, 0:GK].rearrange("p (j k) -> p j k", j=J), identb[:, :],
                              mask[:, None, :].to_broadcast([P, J, NK]), start=False, stop=True)
                last.then_inc(s["s_ok"], 1)

            def probs_t(n, h):
                pe.wait_ge(s["exp_ok"], 2 * n + h + 1)
                for q in range(2):
                    wait(pe, s["pt_used"], 4 * n + 2 * h + q - 1)
                    for j in range(J):
                        at = (q * J + j) * NK
                        t = pe.transpose(PTp[0:NK, q, j * P:(j + 1) * P], PR[:, h, at:at + NK], ident[:, :])
                    t.then_inc(s["pt_ok"], 1)

            def fill(full, read, t):
                wait(pe, s[read], t - 1)

            def body(l, b, k, q):
                n, p, at = NB * l + b, k % 2, (l, b, k, q)
                if here(b):
                    scores(*at, 1)
                if here(b - 1):
                    pe.wait_ge(s["pt_used"], 4 * n)
                    pe.wait_ge(s["vp_ok"], n)
                    fill("b_full", "b_read", b_turn(*at, "pv"))
                    for i in range(2):
                        for j in range(J):
                            for g in range(G):
                                v = mm(B[32 * g:32 * g + 32, i * P:(i + 1) * P],
                                       OV[:, 32 * j:32 * j + 32] if i else VP[:, 1 - p, g, 32 * j:32 * j + 32],
                                       PT[:, 1 - p, (g * J + j) * P:(g * J + j + 1) * P],
                                       start=(j == 0), stop=(j == J - 1))
                    v.then_inc(s["b_full"], 1)
                if here(b):
                    probs_t(n, 0)
                if here(b + 2):
                    pe.wait_ge(s["xn_ok"], n + 3)
                    pe.wait_ge(ctx_ld[(k + 2) % 4], 16 * (4 * l + q + (k + 2) // 4 + 1))
                    fill("a_full", "a_read", a_turn(*at, "xc"))
                    pe.transpose(A[:, 0:P], xn[:, p, :], ident[:, :])
                    pe.transpose(A[:, P:P + NK], ctx[:, (k + 2) % 4, :], ident[0:NK, 0:NK]).then_inc(s["a_full"], 1)
                if here(b + 1):
                    scores(l, b + 1, (k + 1) % 4, q + (k + 1) // 4, 0)
                if l and (here(b + 2) or here(b + 1)):
                    pe.wait_ge(s["proj_ld"], 16 * 6)
                    fill("a_full", "a_read", a_turn(*at, "qkv"))
                    if here(b + 2):
                        mm(A[:, 0:P], wq_sb[:, :], xT[:, p, :], start=True, stop=True)
                        v = mm(A[:, P:P + NK], wk_sb[:, :], cT[:, p, :], start=True, stop=True)
                    if here(b + 1):
                        v = mm(A[0:NK, 2 * P:3 * P], cT[:, 1 - p, :], wv_sb[:, :], start=True, stop=True)
                    v.then_inc(s["a_full"], 1)
                if here(b - 1):
                    fill("b_full", "b_read", b_turn(*at, "proj"))
                    if l == 0:
                        mm(B[:, 0:D], ones_f[0:1, :], bfc_sb[0:1, :], start=True, stop=False)
                    mm(B[:, 0:D], OT[:, 1 - p, :], wt_sb[:, :] if l else wfcT[:, :],
                       start=bool(l), stop=True).then_inc(s["b_full"], 1)
                if here(b):
                    probs_t(n, 1)
                if here(b - 2) or here(b - 3):
                    fill("a_full", "a_read", a_turn(*at, "gl"))
                    if here(b - 2):
                        pe.wait_ge(s["xg_ok"], n - 1)
                        v = pe.transpose(A[:, 0:P], xg[:, p, :], ident[:, :])
                    if here(b - 3):
                        pe.wait_ge(s["proj_ld"], 16 * 6)
                        v = mm(A[:, P:P + E], xgT[:, 1 - p, :], gate[l][:, :], start=True, stop=True)
                    v.then_inc(s["a_full"], 1)
                if k == 3 and here(b - 7):
                    quad = 4 * l + q - 1
                    pe.wait_ge(s["ohb_ok"], quad + 1)
                    wait(pe, s["consts_ok"], 1)
                    fill("b_full", "b_read", b_turn(*at, "prefix"))
                    mm(B[:, 0:QT * E], before[:, :], OHB[:, :, :], start=True, stop=False)
                    for d in range(1, QT):
                        mm(B[:, d * E:QT * E], onesb[:, :], OHB[:, 0:QT - d, :], start=False, stop=False)
                    mm(B[:, 0:QT * E].rearrange("p (t e) -> p t e", t=QT), onesb[:, :],
                       OHacc[:, None, :].to_broadcast([P, QT, E]), start=False, stop=True).then_inc(s["b_full"], 1)

            pe.wait_ge(s["wfc_ld"], 32)
            pe.wait_ge(s["ident_ok"], 1)
            pe.transpose(A[:, 0:P], wfc_sb[:, :], ident[:, :]).then_inc(s["a_full"], 1)
            for l in range(2):
                over_batches(pe, l, body)
                pe.wait_ge(s["r3"], R3N[0] * 4 + l * R3N[1] * 4)
                fill("b_full", "b_read", counts_turn(l))
                mm(B[:, 0:E], onesb[:, :], OHacc[:, :], start=True, stop=True).then_inc(s["b_full"], 1)
                pe.wait_ge(s["tables_ok"], l + 1)
                pe.wait_ge(s["bias_parts"], 16 * 12)
                pe.wait_ge(s["w_ok"], W_ALL)
                nf = FF[l] // P
                word = [None]

                def expert(word, k, i):
                    return (word >> EBITS * (k + i)) & (E - 1)

                def tile(l, r, k, j):
                    m = T0[l] + r
                    if k == 0 or (isinstance(r, int) and r == -2):
                        word[0] = pe.value_load(TE[l][0:1, bass.ds(j + 1, 1)], min_val=0, max_val=E ** WORD - 1)
                    if tile_here(l, r + 1):
                        e = expert(word[0], k, 2)
                        pe.wait_ge(s["xtT_used"], m + 2)
                        wait(pe, s["h_used"], m)
                        h = S[:, (k + 1) % 2, 0:FF[l]]
                        mm(h, onesb[0:3, :], b1s[l][:, bass.ds(e * FF[l], FF[l])], start=True, stop=False)
                        mm(h, xtT[:, (k + 1) % 2, :], W1[l][:, bass.ds(e * FF[l], FF[l])],
                           start=False, stop=True).then_inc(s["h_ok"], 1)
                    if tile_here(l, r + 2):
                        kk = (k + 2) % 4
                        pe.wait_ge(xt_ld[kk], (j + (k + 2) // 4 + SLOT0[l][kk] + 1) * 16)
                        wait(pe, s["xtT_used"], m + 2)
                        pe.transpose(A[:, 0:P], xt[:, kk, :], ident[:, :]).then_inc(s["xtT_ok"], 1)
                    if tile_here(l, r):
                        pe.wait_ge(s["h_used"], m + 1)
                        wait(pe, s["hT_used"], m - 1)
                        for c in range(nf):
                            v = pe.transpose(S[:, 2 + k % 2, c * P:(c + 1) * P], H[:, k % 2, c * P:(c + 1) * P], ident[:, :])
                        v.then_inc(s["hT_ok"], 1)
                    if tile_here(l, r - 1):
                        e = expert(word[0], k, 0)
                        pe.wait_ge(s["hT_used"], m)
                        wait(pe, s["y_used"], m - 2)
                        y = PTp[:, (k + 1) % 2, 0:D]
                        mm(y, onesb[0:3, :], b2s[l][:, bass.ds(e * D, D)], start=True, stop=False)
                        for c in range(nf):
                            v = mm(y, HT[:, (k + 1) % 2, c * P:(c + 1) * P], W2[l][:, bass.ds(e * FF[l] + c * P, D)],
                                   start=False, stop=(c == nf - 1))
                        v.then_inc(s["y_ok"], 1)

                over_tiles(pe, l, tile, 2, 1)
                done = T0[l] + TILES[l]
                for name in ("hT_used", "h_used", "y_used", "xtT_used"):
                    pe.wait_ge(s[name], done)

        @block.vector
        def _(dve):
            tt, ts, cp = dve.tensor_tensor, dve.tensor_scalar, dve.tensor_copy

            def halves(h):
                return S[:, 2 * h:2 * h + 2, 0:GK].rearrange("p g (j k) -> p g j k", j=J)

            def max_sub(n, h):
                dve.wait_ge(s["s_ok"], 2 * n + h + 1)
                wait(dve, s["exp_ok"], 2 * n + h - 1)
                m = M[:, h, :].rearrange("p (g j) -> p g j", g=2)
                dve.tensor_reduce(m, halves(h), AX_X, ALU.max).then_inc(s["m_ok"], 1)
                dve.wait_ge(s["m_ok"], 2 * n + h + 1)
                tt(SB[:, h, :].rearrange("p (g j k) -> p g j k", g=2, j=J), halves(h),
                   m[:, :, :, None].to_broadcast([P, 2, J, NK]), ALU.subtract).then_inc(s["sub_ok"], 1)

            def hold():
                dve.sem_inc(s["held"], 1)

            def stats(src, n, p, k, st, mv, st_ok, mv_ok):
                hold()
                dve.bn_stats(st[:, p, :], src).then_inc(s[st_ok], 1)
                dve.wait_ge(s[st_ok], n + 1)
                hold()
                dve.bn_aggr(mv[:, k, :], st[:, p, :]).then_inc(s[mv_ok], 1)

            def combine(l, b, k, q):
                dve.wait_ge(gath[k], (TOPK[l] * (q + 1) + l * TOPK[0] * 4) * 16)
                for c in range(TOPK[l]):
                    lastc = c == TOPK[l] - 1
                    if c:
                        dve.wait_ge(s["comb_part"], b + 1)
                    dve.scalar_tensor_tensor(out=X[:, b, :], in0=YG[:, k, c, :], scalar=GV[l][:, c, bass.ds(b, 1)],
                                             in1=X[:, b, :], op0=ALU.mult, op1=ALU.add)\
                        .then_inc(s["combined" if lastc else "comb_part"], 1)

            def chain(name, base):
                count = [0]

                def link(ins):
                    count[0] += 1
                    ins.then_inc(s[name], 1)
                    dve.wait_ge(s[name], base + count[0])
                return link, count

            def route1(l, quad):
                link, c = chain("r1", quad * R1N)
                link(dve.tensor_reduce(rmax[:, :], LG[:, :, :], AX_X, ALU.max))
                link(tt(rsub[:, :, :], LG[:, :, :], rmax[:, :, None].to_broadcast([P, QT, E]), ALU.subtract))
                assert c[0] == R1N

            def over_e(v):
                return v[:, :, None].to_broadcast([P, QT, E])

            def route2(l, quad, t0, part):
                start = (0, 6, 12 if TOPK[l] == 2 else 8)[part]
                stop = (6, 12 if TOPK[l] == 2 else 8, R2N[l])[part]
                link, c = chain("r2", (quad * R2N[l] if l == 0 else (quad - 4) * R2N[1] + 4 * R2N[0]) + start)

                def oh(k):
                    return OH[:, k, bass.ds(t0, QT), :]

                def best(k, pk):
                    link(dve.tensor_reduce(val[:, k, :], pk[:, :, :], AX_X, ALU.max))
                    link(tt(eq[:, :, :], pk[:, :, :], over_e(val[:, k, :]), ALU.is_equal))
                    link(tt(rank[:, :, :], eq[:, :, :], revf[:, :, :], ALU.mult))

                def chosen(k):
                    link(dve.tensor_reduce(first[:, :], rank[:, :, :], AX_X, ALU.max))
                    link(tt(oh(k), revf[:, :, :], over_e(first), ALU.is_equal))

                if part == 0:
                    dve.wait_ge(s["rexp_ok"], quad + 1)
                    dve.wait_ge(s["consts_ok"], 1)
                    link(dve.tensor_reduce(rsum[:, :], rexp[:, :, :], AX_X, ALU.add))
                    link(dve.reciprocal(rrec[:, :], rsum[:, :]))
                    link(tt(prob[:, :, :], rexp[:, :, :], over_e(rrec), ALU.mult))
                    best(0, prob)
                if part == 1:
                    chosen(0)
                    if TOPK[l] == 2:
                        link(dve.scalar_tensor_tensor(out=prob2[:, :, :], in0=oh(0), scalar=-2.0,
                                                      in1=prob[:, :, :], op0=ALU.mult, op1=ALU.add))
                        best(1, prob2)
                if part == 2 and TOPK[l] == 2:
                    chosen(1)
                    tt(OHB[:, :, :], oh(0), oh(1), ALU.add).then_inc(s["ohb_ok"], 1)
                    link(tt(gden[:, :], val[:, 0, :], val[:, 1, :], ALU.add))
                    link(ts(gden[:, :], gden[:, :], 1e-12, None, ALU.max))
                    link(dve.reciprocal(gden[:, :], gden[:, :]))
                    link(tt(GV[l][:, :, bass.ds(t0, QT)], val[:, :, :], gden[:, None, :].to_broadcast([P, 2, QT]), ALU.mult))
                if part == 2 and TOPK[l] == 1:
                    ts(OHB[:, :, :], oh(0), 1.0, None, ALU.mult).then_inc(s["ohb_ok"], 1)
                    link(ts(GV[l][:, 0, bass.ds(t0, QT)], val[:, 0, :], 1.0, None, ALU.mult))
                assert start + c[0] == stop, c

            def route3(l, quad, t0, turn_no):
                link, c = chain("r3", quad * R3N[0] if l == 0 else (quad - 4) * R3N[1] + 4 * R3N[0])
                dve.wait_ge(s["b_full"], turn_no)
                tt(pos[:, :, :], B[:, 0:QT * E].rearrange("p (t e) -> p t e", t=QT), region0[:, :, :],
                   ALU.add).then_inc(s["b_read"], 1)
                dve.wait_ge(s["b_read"], turn_no)
                for k in range(TOPK[l]):
                    link(tt(posk[:, :, :], pos[:, :, :], OH[:, k, bass.ds(t0, QT), :], ALU.mult))
                    link(dve.tensor_reduce(POSF[:, k, bass.ds(t0, QT)], posk[:, :, :], AX_X, ALU.add))
                    ins = ts(IDX[l][:, k, bass.ds(t0, QT)], POSF[:, k, bass.ds(t0, QT)], 1.0, None, ALU.mult)
                    if k == TOPK[l] - 1:
                        ins.then_inc(s["idx_ok"], 1)
                    else:
                        link(ins)
                link(dve.tensor_reduce(ohsum[:, :], OHB[:, :, :].rearrange("p t e -> p e t"), AX_X, ALU.add))
                link(tt(OHacc[:, :], OHacc[:, :], ohsum[:, :], ALU.add))
                dve.wait_ge(s["idx_ok"], quad + 1)
                assert c[0] == R3N[l], c

            def keys(n, p, l, t):
                dve.wait_ge(s["a_read"], t)
                wait(dve, s["s_ok"], 2 * n + 2)
                src = kTs if l else cT
                tt(KB[:, p, :].rearrange("p (j k) -> p j k", j=J), src[:, p, None, :].to_broadcast([P, J, NK]),
                   own[:, :, None].to_broadcast([P, J, NK]), ALU.mult).then_inc(s["kb_ok"], 1)

            def row(t):
                return X[:, bass.ds(t, 1), :].rearrange("p a d -> p (a d)")

            def body(l, b, k, q):
                n, p, at = NB * l + b, k % 2, (l, b, k, q)
                if here(b):
                    max_sub(n, 1)
                if k == 3 and here(b - 7):
                    route2(l, 4 * l + q - 1, (q - 1) * QT, 0)
                if here(b + 2):
                    kk = (k + 2) % 4
                    dve.wait_ge(s["rstd1_ok"], n + 3)
                    ts(xn[:, p, :], row(b + 2), mv1[:, kk, 0:1], rstd1[:, kk:kk + 1],
                       ALU.subtract, ALU.mult).then_inc(s["xn_ok"], 1)
                if here(b - 1):
                    dve.wait_ge(s["b_full"], b_turn(*at, "pv"))
                    dve.reciprocal(total[:, :], B[:, P:2 * P]).then_inc(s["total_ok"], 1)
                    dve.wait_ge(s["total_ok"], n)
                    tt(OT[:, 1 - p, :], B[:, 0:P], total[:, :], ALU.mult).then_inc(s["b_read"], 1)
                    dve.sem_inc(s["pv_done"], 1)
                if here(b + 2) and not l:
                    keys(n, p, l, a_turn(*at, "xc"))
                if here(b - 2):
                    dve.wait_ge(s["rstd2_ok"], n - 1)
                    if here(b - 4) and not here(b + 1):
                        dve.wait_ge(s["a_full"], a_turn(l, b - 2, (k - 2) % 4, q - (k < 2), "gl"))
                    kk = (k - 2) % 4
                    ts(xg[:, p, :], row(b - 2), mv2[:, kk, 0:1], rstd2[:, kk:kk + 1],
                       ALU.subtract, ALU.mult).then_inc(s["xg_ok"], 1)
                if k == 3 and here(b - 7):
                    route2(l, 4 * l + q - 1, (q - 1) * QT, 1)
                if here(b + 1):
                    max_sub(n + 1, 0)
                if k == 3 and here(b - 7):
                    route2(l, 4 * l + q - 1, (q - 1) * QT, 2)
                if here(b + 2) and l:
                    keys(n, p, l, a_turn(*at, "qkv"))
                if here(b - 1):
                    dve.wait_ge(s["b_full"], b_turn(*at, "proj"))
                    xb = row(b - 1)
                    tt(xb, B[:, 0:D], xb, ALU.add).then_inc(s["b_read"], 1)
                    dve.wait_ge(s["b_read"], b_turn(*at, "proj"))
                    wait(dve, s["xn2_ok"], n - 4)
                    stats(xb, n - 1, 1 - p, (k - 1) % 4, st2, mv2, "st2_ok", "mv2_ok")
                if here(b + 3):
                    kk = (k + 3) % 4
                    if l:
                        combine(0, b + 3, kk, q + (k + 3) // 4)
                        dve.wait_ge(s["combined"], b + 4)
                    else:
                        dve.wait_ge(x_ld[0], 16)
                        if not isinstance(b, int) or b + 3 >= 4:
                            dve.wait_ge(x_ld[1], 16)
                    stats(row(b + 3), n + 3, 1 - p, kk, st1, mv1, "st1_ok", "mv1_ok")
                if k == 2 and here(b - 6):
                    dve.wait_ge(s["a_read"], a_turn(*at, "gl"))
                    route1(l, 4 * l + q - 1)
                if k == 3 and here(b - 7):
                    route3(l, 4 * l + q - 1, (q - 1) * QT, b_turn(*at, "prefix"))

            def tables(l):
                link, c = chain("tab", l * TABN[0])

                def experts(i, nw):
                    return tef[:, i:i + 4 * nw].rearrange("p (w t) -> p w t", t=4)[:, :, 0]
                nt = TILES[l]
                dve.wait_ge(s["b_full"], counts_turn(l))
                cp(cnt[:, :], B[:, 0:E]).then_inc(s["b_read"], 1)
                dve.wait_ge(s["b_read"], counts_turn(l))
                link(ts(cnti[:, :], cnt[:, :], float(P - 1), None, ALU.add))
                link(ts(nti[:, :], cnti[:, :], 7, None, ALU.arith_shift_right))
                link(cp(ntf[:, :], nti[:, :]))
                link(cp(cum[:, 0, 4:], nti[:, :]))
                for i, d in enumerate((1, 2, 4)):
                    link(tt(cum[:, i + 1, 4:], cum[:, i, 4:], cum[:, i, 4 - d:4 + E - d], ALU.add))
                total = cum[0:1, 3, 3 + E:4 + E]
                shape = [1, nt, E - 1]
                link(tt(ge[:, 0:nt, :], tile_no[:, 0:nt, :], cum[0:1, 3, None, 4:3 + E].to_broadcast(shape), ALU.is_ge))
                link(dve.tensor_reduce(tef[:, WORD - 1:WORD - 1 + nt], ge[:, 0:nt, :], AX_X, ALU.add))
                link(tt(gen[:, 0:nt, :], ge[:, 0:nt, :], ntf[0:1, None, 0:E - 1].to_broadcast(shape), ALU.mult))
                link(dve.tensor_reduce(startf[:, 0:nt], gen[:, 0:nt, :], AX_X, ALU.add))
                link(ts(validf[:, 0:nt], tile_no[:, 0:nt, 0], total, None, ALU.is_lt))
                link(tt(offf[:, 0:nt], tile_no[:, 0:nt, 0], startf[:, 0:nt], ALU.subtract))
                link(dve.scalar_tensor_tensor(out=offf[:, 0:nt], in0=offf[:, 0:nt], scalar=float(P), in1=validf[:, 0:nt],
                                              op0=ALU.mult, op1=ALU.mult))
                link(dve.scalar_tensor_tensor(out=rowf[:, 0:nt], in0=tef[:, WORD - 1:WORD - 1 + nt], scalar=float(REGION), in1=offf[:, 0:nt],
                                              op0=ALU.mult, op1=ALU.add))
                link(cp(ROW[l][:, :], rowf[:, 0:nt]))
                nw = NW[l]
                link(cp(packf[:, 0:nw], experts(WORD - 1, nw)))
                for i in range(WORD - 2, -1, -1):
                    link(dve.scalar_tensor_tensor(out=packf[:, 0:nw], in0=packf[:, 0:nw], scalar=float(E),
                                                  in1=experts(i, nw), op0=ALU.mult, op1=ALU.add))
                link(cp(TE[l][:, :], packf[:, 0:nw]))
                link(tt(fillf[:, :], cnt[0:1, :], region0[0:1, 0, :], ALU.add))
                cp(FILL[l][:, :], fillf[:, :]).then_inc(s["tables_ok"], 1)
                link(dve.memset(OHacc[:, :], 0.0))
                link(tt(shift[:, :], cum[:, 3, 4:], ntf[:, :], ALU.subtract))
                link(dve.scalar_tensor_tensor(out=shift[:, :], in0=shift[:, :], scalar=float(P), in1=region0[:, 0, :],
                                              op0=ALU.mult, op1=ALU.subtract))
                for k in range(TOPK[l]):
                    link(tt(moved[:, :, :], OH[:, k, :, :], shift[:, None, :].to_broadcast([P, NB, E]), ALU.mult))
                    link(dve.tensor_reduce(movedr[:, :], moved[:, :, :], AX_X, ALU.add))
                    link(tt(movedr[:, :], movedr[:, :], POSF[:, k, :], ALU.add))
                    link(cp(IDXG[l][:, k, :], movedr[:, :]))
                dve.sem_inc(s["idxg_ok"], 1)
                assert c[0] == TABN[l], c

            for l in range(2):
                over_batches(dve, l, body)
                tables(l)

                def tile(l, r, k, j):
                    m = T0[l] + r
                    if tile_here(l, r):
                        dve.wait_ge(s["hT_ok"], m + 1)
                        wait(dve, s["y_ok"], m - 1)
                        cp(HT[:, k % 2, 0:FF[l]], S[:, 2 + k % 2, 0:FF[l]]).then_inc(s["hT_used"], 1)
                    if tile_here(l, r - 1):
                        kk = (k - 1) % 4
                        dve.wait_ge(s["y_ok"], m)
                        wait(dve, y_st[kk], (j + (k - 1) // 4 + SLOT0[l][kk]) * 16)
                        cp(Y[:, kk, :], PTp[:, kk % 2, 0:D]).then_inc(s["y_used"], 1)

                over_tiles(dve, l, tile, 2, 1)
            for b in range(NB):
                combine(1, b, b % 4, b // 4)


_INS = ['x', 'ctx_1024', 'mask_Bx1xSxS2_ik1', 'mask_1x1xSxS2_if1', 'L0_xattn_W_fc', 'L0_xattn_b_fc', 'L0_ffn_gate',
        'L0_ffn_W1', 'L0_ffn_b1', 'L0_ffn_W2', 'L0_ffn_b2', 'L1_xattn_W_Q', 'L1_xattn_W_K', 'L1_xattn_W_V',
        'L1_xattn_W_T', 'L1_ffn_gate_w', 'L1_ffn_w1', 'L1_ffn_b1', 'L1_ffn_w2', 'L1_ffn_b2']


def kernel(**inputs):
    import numpy as _np
    import concourse.bacc as _bacc
    from concourse import mybir as _mybir
    from concourse.bass_utils import run_bass_kernel_spmd as _run

    nc = _bacc.Bacc("TRN2", target_bir_lowering=False, num_devices=1)
    arrays, args = {}, []
    for name in _INS:
        a = _np.ascontiguousarray(inputs[name])
        arrays[f"in_{name}_dram"] = a
        args.append(nc.dram_tensor(f"in_{name}_dram", a.shape, _mybir.dt.from_np(a.dtype), kind="ExternalInput").ap())
    args.append(nc.dram_tensor("out_dram", (16, 128, 128), _mybir.dt.float32, kind="ExternalOutput").ap())
    build(nc, *args)
    r = _run(nc, [arrays], core_ids=[0])
    return r.results[0]["out_dram"]
```

```python
from contextlib import ExitStack

import concourse.bass as bass
from concourse import mybir

F32 = mybir.dt.float32
BF16 = mybir.dt.bfloat16
I32 = mybir.dt.int32
U32 = mybir.dt.uint32
ALU = mybir.AluOpType
ACT = mybir.ActivationFunctionType
AX_X = mybir.AxisListType.X

P = 128
NB = 16
D = 128
NH = 16
DH = D // NH
NK = 77
G = 4
J = NH // G
GK = J * NK
E = 8
QT = 4
REGION = NB * P + P
SPARE = E * REGION
MASKED = 1e20
EPS = 1e-5
FF = (256, 512)
TOPK = (2, 1)
TILES = tuple(NB * k + E - 1 for k in TOPK)
EBITS = E.bit_length() - 1
WORD = 6
NW = tuple(t // 4 + 2 for t in TILES)
ROW_LEN = (D, 2 * D + 2)
SCALE = (float(D) ** -0.5, float(DH) ** -0.5)


def wait(eng, sem, value):
    if not isinstance(value, int) or value > 0:
        eng.wait_ge(sem, value)


def here(b):
    return not isinstance(b, int) or 0 <= b < NB


def build(nc, x, ctx_in, mask0, mask1, wfc, bfc, gate0, w1_0, b1_0, w2_0, b2_0,
          wq, wk, wv, wt, gate1, w1_1, b1_1, w2_1, b2_1, out):
    xs = [nc.dram_tensor(f"sorted_rows{l}", (SPARE + P, ROW_LEN[l]), F32).ap() for l in range(2)]
    ys = nc.dram_tensor("sorted_outputs", (TILES[0] * P, D), F32).ap()
    out_rows = out.rearrange("b p d -> (b p) d")
    with ExitStack() as stack:
        def sb(name, shape, dt=F32):
            return stack.enter_context(nc.sbuf_tensor(name, shape, dt))

        def pb(name, shape, dt=F32):
            return stack.enter_context(nc.psum_tensor(name, shape, dt))

        def sem(name):
            return stack.enter_context(nc.semaphore(name))

        X = sb("X", [P, NB, D])
        W1 = [sb(f"W1_{l}", [P, E * FF[l]]) for l in range(2)]
        W2 = [sb(f"W2_{l}", [P, E * FF[l]]) for l in range(2)]
        b1row = [sb(f"b1row{l}", [E, FF[l]]) for l in range(2)]
        b2row = [sb(f"b2row{l}", [E, D]) for l in range(2)]
        b1rem = [sb(f"b1rem{l}", [E, 2, FF[l]]) for l in range(2)]
        b2rem = [sb(f"b2rem{l}", [E, 2, D]) for l in range(2)]
        b1part = [sb(f"b1part{l}", [E, 3, FF[l]], BF16) for l in range(2)]
        b2part = [sb(f"b2part{l}", [E, 3, D], BF16) for l in range(2)]
        b1s = [sb(f"b1s{l}", [3, E * FF[l]], BF16) for l in range(2)]
        b2s = [sb(f"b2s{l}", [3, E * D], BF16) for l in range(2)]
        gate = [sb(f"gate{l}", [P, E]) for l in range(2)]
        wfc_sb = sb("wfc_sb", [P, D])
        wfcT = sb("wfcT", [P, D])
        wq_sb, wk_sb, wv_sb, wt_sb = (sb(n, [P, D]) for n in ("wq_sb", "wk_sb", "wv_sb", "wt_sb"))
        bfc_sb = sb("bfc_sb", [1, D])
        ident = sb("ident", [P, P])
        identb = sb("identb", [P, P], BF16)
        ones_f = sb("ones_f", [P, P])
        onesb = sb("onesb", [P, P], BF16)
        before = sb("before", [P, P], BF16)
        own_a = sb("own_a", [P, J])
        own = sb("own", [P, J])
        zeros = sb("zeros", [P, ROW_LEN[1]])
        minus_half = sb("minus_half", [P, 1])
        table_load = sb("table_load", [P, 1])
        region0 = sb("region0", [P, QT, E])
        revf = sb("revf", [P, QT, E])
        iot = sb("iot", [P, QT, E], I32)
        token_i = sb("token_i", [P, NB + 1], I32)
        tile_no_i = sb("tile_no_i", [1, max(TILES), E - 1], I32)
        tile_no = sb("tile_no", [1, max(TILES), E - 1])
        mask0_sb = sb("mask0_sb", [P, NB, NK], I32)
        mask1_sb = sb("mask1_sb", [P, NK], I32)
        ctx = sb("ctx", [NK, QT, D])
        bias = sb("bias", [P, NB, NK], BF16)
        bias1 = sb("bias1", [P, NK], BF16)
        st1 = sb("st1", [P, 2, 6])
        mv1 = sb("mv1", [P, 4, 2])
        ve1 = sb("ve1", [P, 4])
        rstd1 = sb("rstd1", [P, 4])
        st2 = sb("st2", [P, 2, 6])
        mv2 = sb("mv2", [P, 4, 2])
        ve2 = sb("ve2", [P, 4])
        rstd2 = sb("rstd2", [P, 4])
        xn = sb("xn", [P, 2, D])
        xT = sb("xT", [P, 2, P])
        Q = sb("Q", [P, 2, G, P])
        cT = sb("cT", [P, 2, NK])
        kTs = sb("kTs", [P, 2, NK])
        Vs = sb("Vs", [NK, 2, D])
        KB = sb("KB", [P, 2, GK])
        VP = sb("VP", [NK, 2, G, 160])
        M = sb("M", [P, 2, 2 * J])
        SB = sb("SB", [P, 2 * GK])
        PR = sb("PR", [P, 2, 2 * GK])
        PT = sb("PT", [NK, 2, NH * P])
        SUM = sb("SUM", [P, 2, NH])
        R = sb("R", [P, NH])
        RX = sb("RX", [P, D])
        RT = sb("RT", [P, P])
        OT = sb("OT", [P, 2, P])
        XR = sb("XR", [P, NB, ROW_LEN[1]])
        xg = sb("xg", [P, 2, D])
        xgT = sb("xgT", [P, 2, P])
        LG = sb("LG", [P, QT, E])
        rmax = sb("rmax", [P, QT])
        rsub = sb("rsub", [P, QT, E])
        rexp = sb("rexp", [P, QT, E])
        rsum = sb("rsum", [P, QT])
        rrec = sb("rrec", [P, QT])
        prob = sb("prob", [P, QT, E])
        val = sb("val", [P, 2, QT])
        eq = sb("eq", [P, QT, E])
        rank = sb("rank", [P, QT, E])
        first = sb("first", [P, QT])
        OH = sb("OH", [P, 2, NB, E])
        prob2 = sb("prob2", [P, QT, E])
        gden = sb("gden", [P, QT])
        OHB = sb("OHB", [P, QT, E], BF16)
        ohsum = sb("ohsum", [P, E])
        OHacc = sb("OHacc", [P, E], BF16)
        pos = sb("pos", [P, QT, E])
        posk = sb("posk", [P, 2, QT, E])
        POSF = sb("POSF", [P, 2, NB])
        IDX = [sb(f"IDX{l}", [P, 2, NB], I32) for l in range(2)]
        IDXG = sb("IDXG", [P, 2, NB], I32)
        GV = sb("GV", [P, 2, NB])
        cnt = sb("cnt", [P, E])
        cnti = sb("cnti", [P, E], I32)
        nti = sb("nti", [P, E], I32)
        ntf = sb("ntf", [P, E])
        cum = sb("cum", [P, 4, 4 + E])
        ge = sb("ge", [1, max(TILES), E - 1])
        gen = sb("gen", [1, max(TILES), E - 1])
        tef = sb("tef", [1, 4 * max(NW) + WORD - 1])
        packf = sb("packf", [1, max(NW)])
        startf = sb("startf", [1, max(TILES)])
        tel = sb("tel", [1, max(TILES)])
        validf = sb("validf", [1, max(TILES)])
        offf = sb("offf", [1, max(TILES)])
        rowf = sb("rowf", [1, max(TILES)])
        shift = sb("shift", [P, E])
        moved = sb("moved", [P, 2 * NB, E])
        movedr = sb("movedr", [P, 2 * NB])
        fillf = sb("fillf", [1, E])
        TE = [sb(f"TE{l}", [1, NW[l]], I32) for l in range(2)]
        ROW = [sb(f"ROW{l}", [1, TILES[l]], I32) for l in range(2)]
        FILL = [sb(f"FILL{l}", [1, E], I32) for l in range(2)]
        xt = sb("xt", [P, 4, ROW_LEN[1]])
        xtT = sb("xtT", [P, 2, P])
        H = sb("H", [P, 2, max(FF)])
        HT = sb("HT", [P, 2, max(FF)])
        Y = sb("Y", [P, 4, D])
        carried = sb("carried", [P, 4, ROW_LEN[1] - D])
        Ytok = sb("Ytok", [P, 4], I32)
        YG = sb("YG", [P, 4, 2, D])

        S = pb("S", [P, G, 512])
        PTp = pb("PTp", [P, 2, 512])
        A = pb("A", [P, 512])
        B = pb("B", [P, 512])

        names = ("w_ok proj_ld wfc_ld mask_ld bias_ld bias_split bias_parts pool_chain ident_ok consts_ok "
                 "a_full a_read b_full b_read bias_ok vp_ok "
                 "combined comb_part st1_ok mv1_ok ve1_ok rstd1_ok xn_ok "
                 "s_ok m_ok sub_ok sum_ok exp_ok pt_ok pt_used kb_ok recip_ok rx_ok pv_done "
                 "st2_ok mv2_ok ve2_ok rstd2_ok xn2_ok xg_ok r1 rexp_ok r2 r3  ohb_ok idx_ok tab tables_ok idxg_ok "
                 "scattered filled xtT_ok xtT_used h_ok h_used hT_ok hT_used y_ok y_used held q_zero fill_ok carried_ok").split()
        s = {n: sem(n) for n in names}
        ctx_ld = [sem(f"ctx_ld{i}") for i in range(4)]
        x_ld = [sem(f"x_ld{i}") for i in range(2)]
        xt_ld = [sem(f"xt_ld{i}") for i in range(4)]
        y_st = [sem(f"y_st{i}") for i in range(4)]
        out_st = [sem(f"out_st{i}") for i in range(4)]
        gath = [sem(f"gath{i}") for i in range(4)]
        block = stack.enter_context(nc.Block())

        R1N, R2N, R3N, TABN = 2, (14, 8), (8, 5), (30, 24)
        W_ALL = 16 * 2 * (1 + E)
        FIRST, LAST = -3, NB + 5

        def over_batches(eng, l, body):
            for b in range(FIRST, 5):
                body(l, b, b % 4, b // 4)
            with eng.Fori(1, 3) as i:
                for k in range(1, 5):
                    body(l, i * 4 + k, k % 4, i + k // 4)
            for b in range(NB - 3, LAST):
                body(l, b, b % 4, b // 4)

        def over_tiles(eng, l, body, lead, lag):
            n = TILES[l]
            top = (n - lead) // 4 * 4
            for r in range(-lead, 8):
                body(l, r, r % 4, r // 4)
            with eng.Fori(2, top // 4) as i:
                for k in range(4):
                    body(l, i * 4 + k, k, i)
            for r in range(top, n + lag):
                body(l, r, r % 4, r // 4)

        def tile_here(l, r):
            return not isinstance(r, int) or 0 <= r < TILES[l]

        def fill_up(eng, l, experts):
            for e in experts:
                row = eng.value_load(FILL[l][0:1, e:e + 1], min_val=0, max_val=SPARE)
                eng.dma_start(xs[l][bass.ds(row, P), :], zeros[:, 0:ROW_LEN[l]]).then_inc(s["filled"], 16)

        T0 = (0, TILES[0])
        SLOT0 = ([0] * 4, [len(range(k, TILES[0], 4)) for k in range(4)])

        def a_uses(l, b):
            return ((["xc"] if here(b + 2) else []) + (["gl"] if here(b) or here(b - 2) or here(b - 3) else [])
                    + (["qkv"] if l and (here(b + 2) or here(b + 1)) else []))

        def b_uses(l, b):
            return ((["pv", "proj"] if here(b - 1) else [])
                    + (["prefix"] if b % 4 == 0 and 0 <= b - 8 < NB else []))

        def turn(uses, l, b, k, q, stage):
            def at(b):
                n = 1 if uses is a_uses else 0
                if l:
                    n += sum(len(uses(0, c)) for c in range(FIRST, LAST)) + (uses is b_uses)
                n += sum(len(uses(l, c)) for c in range(FIRST, b))
                return n + uses(l, b).index(stage) + 1
            if isinstance(b, int):
                return at(b)
            first = 1 if k else 2
            c = at(4 * first + k)
            d = at(4 * first + 4 + k) - c
            return q * d + (c - first * d)

        def a_turn(*x):
            return turn(a_uses, *x)

        def b_turn(*x):
            return turn(b_uses, *x)

        def counts_turn(l):
            return sum(len(b_uses(i, c)) for i in range(l + 1) for c in range(FIRST, LAST)) + l + 1

        @block.sync
        def _(sp):
            xv = x.rearrange("b p d -> p b d")
            sp.dma_start(X[:, 0:4, :], xv[:, 0:4, :]).then_inc(x_ld[0], 16)

            def load_ctx(l, b, k):
                n = NB * l + b
                wait(sp, s["kb_ok"], n - 3)
                wait(sp, s["vp_ok"], n - 3)
                sp.dma_start(ctx[:, k, :], ctx_in[b, :, :]).then_inc(ctx_ld[k], 16)

            def bias_parts(l):
                sp.wait_ge(s["bias_split"], l + 1)
                for c in range(3):
                    sp.dma_start(b1s[l][c:c + 1, :].rearrange("p (e f) -> p e f", e=E),
                                 b1part[l][:, c, :]).then_inc(s["bias_parts"], 16)
                    sp.dma_start(b2s[l][c:c + 1, :].rearrange("p (e f) -> p e f", e=E),
                                 b2part[l][:, c, :]).then_inc(s["bias_parts"], 16)

            for b in range(4):
                load_ctx(0, b, b)
            sp.dma_start(wfc_sb[:, :], wfc).then_inc(s["wfc_ld"], 16)
            sp.dma_start(bfc_sb[:, :], bfc.rearrange("(a d) -> a d", a=1)).then_inc(s["wfc_ld"], 16)
            sp.dma_start(mask0_sb[:, :, :], mask0.rearrange("b o q k -> q (b o) k")).then_inc(s["mask_ld"], 16)
            sp.dma_start(mask1_sb[:, :], mask1.rearrange("a o q k -> q (a o k)")).then_inc(s["mask_ld"], 16)
            sp.dma_start(X[:, 4:NB, :], xv[:, 4:NB, :]).then_inc(x_ld[1], 16)
            for dst, src in ((gate[0], gate0), (gate[1], gate1), (wq_sb, wq), (wk_sb, wk), (wv_sb, wv), (wt_sb, wt)):
                sp.dma_start(dst[:, :], src).then_inc(s["proj_ld"], 16)
            for l, (b1, b2) in enumerate(((b1_0, b2_0), (b1_1, b2_1))):
                sp.dma_start(b1row[l][:, :], b1).then_inc(s["bias_ld"], 16)
                sp.dma_start(b2row[l][:, :], b2).then_inc(s["bias_ld"], 16)
            for l, (w1, w2) in enumerate(((w1_0, w2_0), (w1_1, w2_1))):
                sp.dma_start(W1[l][:, :].rearrange("p (e f) -> p e f", e=E),
                             w1.rearrange("e d f -> d e f")).then_inc(s["w_ok"], 16)
                for e in range(E):
                    sp.dma_start(W2[l][:, e * FF[l]:(e + 1) * FF[l]].rearrange("p (c d) -> p c d", d=D),
                                 w2[e, :, :].rearrange("(c p) d -> p c d", p=P)).then_inc(s["w_ok"], 16)
            for l in range(2):
                if l:
                    for b in range(4):
                        load_ctx(l, b, b)
                with sp.Fori(1, 4) as i:
                    for k in range(4):
                        load_ctx(l, i * 4 + k, k)
                if l == 0:
                    bias_parts(0)
                sp.wait_ge(s["consts_ok"], 1)
                sp.wait_ge(s["fill_ok"], l + 1)
                fill_up(sp, l, range(0, E, 2))
                sp.dma_start(xs[l][SPARE:SPARE + P, :], zeros[:, 0:ROW_LEN[l]]).then_inc(s["filled"], 16)
                sp.wait_ge(s["tables_ok"], l + 1)
                sp.wait_ge(s["filled"], 16 * (E + 1) * (l + 1))
                sp.wait_ge(s["scattered"], 16 * NB * (TOPK[0] + l * TOPK[1]))

                def tile(l, r, k, j):
                    m = T0[l] + r
                    if tile_here(l, r + 4):
                        row = sp.value_load(ROW[l][0:1, bass.ds(r + 4, 1)], min_val=0, max_val=SPARE)
                        if l:
                            wait(sp, s["carried_ok"], r + 1)
                        else:
                            wait(sp, s["xtT_ok"], r + 1)
                        sp.dma_start(xt[:, k, 0:ROW_LEN[l]], xs[l][bass.ds(row, P), :]).then_inc(xt_ld[k], 16)
                    if l == 0 and tile_here(l, r - 2):
                        sp.wait_ge(s["y_used"], m - 1)
                        sp.dma_start(ys[bass.ds((r - 2) * P, P), :], Y[:, (k - 2) % 4, :]).then_inc(y_st[(k - 2) % 4], 16)

                over_tiles(sp, l, tile, 4, 2)
                if l == 0:
                    bias_parts(1)
            for k in range(4):
                sp.wait_ge(out_st[k], 16 * len(range(k, TILES[1], 4)))

        @block.gpsimd
        def _(pool):
            count = [0]

            def link(ins):
                count[0] += 1
                ins.then_inc(s["pool_chain"], 1)
                pool.wait_ge(s["pool_chain"], count[0])

            link(pool.memset(ones_f[:, :], 1.0))
            link(pool.memset(minus_half[:, :], -0.5))
            pool.affine_select(out=ident[:, :], in_=ones_f[:, :], compare_op=ALU.is_equal, fill=0.0, base=0,
                               pattern=[[-1, P]], channel_multiplier=1).then_inc(s["ident_ok"], 1)
            pool.wait_ge(s["ident_ok"], 1)
            link(pool.tensor_copy(identb[:, :], ident[:, :]))
            for g in range(G):
                rows = slice(32 * g, 32 * g + 32)
                link(pool.affine_select(out=own_a[rows, :], in_=ones_f[rows, 0:J], compare_op=ALU.is_ge, fill=0.0,
                                        base=0, pattern=[[-DH, J]], channel_multiplier=1))
                link(pool.affine_select(out=own[rows, :], in_=own_a[rows, :], compare_op=ALU.is_ge, fill=0.0,
                                        base=DH - 1, pattern=[[DH, J]], channel_multiplier=-1))

            def constants():
                link(pool.memset(zeros[:, :], 0.0))
                link(pool.iota(token_i[:, :], pattern=[[P, NB + 1]], base=0, channel_multiplier=1))
                link(pool.tensor_copy(XR[:, :, 2 * D + 1], token_i[:, 0:NB]))
                link(pool.tensor_copy(zeros[:, 2 * D + 1:2 * D + 2], token_i[:, NB:NB + 1]))
                link(pool.memset(OHacc[:, :], 0.0))
                link(pool.memset(cum[:, :, :], 0.0))
                link(pool.memset(tef[:, :], 0.0))
                link(pool.tensor_copy(onesb[:, :], ones_f[:, :]))
                link(pool.affine_select(out=before[:, :], in_=onesb[:, :], compare_op=ALU.is_gt, fill=0.0, base=0,
                                        pattern=[[1, P]], channel_multiplier=-1))
                link(pool.iota(iot[:, :, :], pattern=[[0, QT], [REGION, E]], base=0, channel_multiplier=0))
                link(pool.tensor_copy(region0[:, :, :], iot[:, :, :]))
                link(pool.iota(iot[:, :, :], pattern=[[0, QT], [-1, E]], base=E, channel_multiplier=0))
                link(pool.tensor_copy(revf[:, :, :], iot[:, :, :]))
                link(pool.iota(tile_no_i[:, :, :], pattern=[[1, max(TILES)], [0, E - 1]], base=0, channel_multiplier=0))
                pool.tensor_copy(tile_no[:, :, :], tile_no_i[:, :, :]).then_inc(s["consts_ok"], 1)

            def split_bias(l, i):
                row, rem, part = (b1row[l], b1rem[l], b1part[l]) if i < 5 else (b2row[l], b2rem[l], b2part[l])
                c, c2 = i % 5 // 2, i % 2 if i < 5 else (i - 5) % 2
                rest = rem[:, c - 1, :] if c else row[:, :]
                if c2:
                    link(pool.tensor_tensor(rem[:, c, :], rest, part[:, c, :], ALU.subtract))
                else:
                    link(pool.tensor_copy(part[:, c, :], rest))
                if i == 9:
                    pool.sem_inc(s["bias_split"], 1)

            def rstd(n, k, mv, ve, rs, mv_ok, ve_ok, rs_ok):
                pool.wait_ge(s[mv_ok], n + 1)
                pool.tensor_scalar(ve[:, k:k + 1], mv[:, k, 1:2], EPS, None, ALU.add).then_inc(s[ve_ok], 1)
                pool.wait_ge(s[ve_ok], n + 1)
                pool.tensor_tensor(rs[:, k:k + 1], ve[:, k:k + 1], minus_half[:, :], ALU.pow).then_inc(s[rs_ok], 1)

            def body(l, b):
                n, p = NB * l + b, b % 2
                if here(b):
                    if l:
                        pool.wait_ge(s["a_read"], a_turn(l, b - 1, (b - 1) % 4, (b - 1) // 4, "qkv"))
                    else:
                        pool.wait_ge(ctx_ld[b % 4], 16 * (b // 4 + 1))
                    wait(pool, s["pv_done"], n - 1)
                    values = Vs[:, p, :] if l else ctx[:, b % 4, :]
                    for g in range(G):
                        v = pool.tensor_copy(VP[:, p, g, :].rearrange("k (j c) -> k j c", c=40)[:, :, 0:DH],
                                             values[:, 32 * g:32 * g + 32].rearrange("k (j c) -> k j c", c=DH))
                    v.then_inc(s["vp_ok"], 1)
                if here(b - 2):
                    t, k = b - 2, (b - 2) % 4
                    pool.wait_ge(s["rstd2_ok"], n - 1)
                    pool.tensor_scalar(XR[:, t, 0:D], XR[:, t, D:2 * D] if l else X[:, t, :], mv2[:, k, 0:1], rstd2[:, k:k + 1],
                                       ALU.subtract, ALU.mult).then_inc(s["xn2_ok"], 1)
                if here(b + 3):
                    wait(pool, s["xn_ok"], n)
                    rstd(n + 3, (b + 3) % 4, mv1, ve1, rstd1, "mv1_ok", "ve1_ok", "rstd1_ok")
                if here(b - 1):
                    wait(pool, s["xg_ok"], n - 4)
                    rstd(n - 1, (b - 1) % 4, mv2, ve2, rstd2, "mv2_ok", "ve2_ok", "rstd2_ok")
                for t in {1: [b - 9, b - 8], 2: [b - 8], 3: [b - 8], 0: []}[b % 4] if b >= 9 else []:
                    pool.wait_ge(s["idx_ok"], 4 * l + t // 4 + 1)
                    pool.wait_ge(s["xn2_ok"], NB * l + t + 1)
                    for k in range(TOPK[l]):
                        pool.indirect_dma_start(
                            out=xs[l], out_offset=bass.IndirectOffsetOnAxis(ap=IDX[l][:, k, t:t + 1].bitcast(U32), axis=0),
                            in_=XR[:, t, 0:ROW_LEN[l]], in_offset=None).then_inc(s["scattered"], 16)

            def gather(t):
                wait(pool, s["combined"], t - 3)
                for k in range(TOPK[0]):
                    pool.indirect_dma_start(
                        out=YG[:, t % 4, k, :], out_offset=None, in_=ys,
                        in_offset=bass.IndirectOffsetOnAxis(ap=IDXG[:, k, t:t + 1].bitcast(U32), axis=0),
                    ).then_inc(gath[t % 4], 16)

            for l in range(2):
                for b in range(FIRST, NB + 9):
                    if l and b == FIRST:
                        for t in range(2):
                            gather(t)
                    body(l, b)
                    if l == 0 and b == FIRST:
                        pool.memset(Q[:, :, :, :], 0.0).then_inc(s["q_zero"], 1)
                        link(pool.memset(VP[:, :, :, :], 0.0))
                    if l == 0 and b == 0:
                        constants()
                    if l == 0 and b == 2:
                        pool.wait_ge(s["bias_ld"], 64)
                    if l == 0 and 3 <= b < 13:
                        split_bias(0, b - 3)
                    if l and b + 5 < NB:
                        gather(b + 5)
                if l == 0:
                    for i in range(10):
                        split_bias(1, i)
                    pool.wait_ge(s["idxg_ok"], 1)
                    for k in range(4):
                        pool.wait_ge(y_st[k], 16 * SLOT0[1][k])
            for r in range(TILES[1]):
                pool.wait_ge(s["y_used"], T0[1] + r + 1)
                pool.indirect_dma_start(
                    out=out_rows, out_offset=bass.IndirectOffsetOnAxis(ap=Ytok[:, r % 4:r % 4 + 1].bitcast(U32), axis=0),
                    in_=Y[:, r % 4, :], in_offset=None, bounds_check=NB * P - 1, oob_is_err=False).then_inc(out_st[r % 4], 16)

        @block.scalar
        def _(act):
            def exps(n, p, h):
                wait(act, s["pt_ok"], 4 * n + 2 * h - 2)
                if h:
                    act.wait_ge(s["sub_ok"], n + 1)
                    wait(act, s["sum_ok"], n)
                    last = act.activation(PR[:, 1, :], SB[:, :], ACT.Exp, scale=-1.0)
                else:
                    act.wait_ge(s["m_ok"], 2 * n + 1)
                    wait(act, s["recip_ok"], n - 1)
                    for j in range(2 * J):
                        last = act.activation(PR[:, 0, j * NK:(j + 1) * NK], S[:, j // J, j % J * NK:(j % J + 1) * NK],
                                              ACT.Exp, bias=M[:, 0, j:j + 1], scale=-1.0, accum_out=SUM[:, p, j:j + 1])
                last.then_inc(s["exp_ok"], 1)

            def probs_out(n, p, h):
                wait(act, s["pv_done"], n - 1)
                for q in range(2):
                    wait(act, s["pt_ok"], 4 * n + 2 * h + q + 1)
                    at = (2 * h + q) * J * P
                    act.copy(PT[:, p, at:at + J * P], PTp[0:NK, q, :]).then_inc(s["pt_used"], 1)

            def queries(l, p):
                for g in range(G):
                    rows = slice(32 * g, 32 * g + 32)
                    act.activation(Q[rows, p, g, :], A[rows, 0:P], ACT.Copy, scale=-SCALE[l])

            def body(l, b, k, q):
                n, p, at = NB * l + b, k % 2, (l, b, k, q)
                if here(b):
                    exps(n, p, 1)
                    probs_out(n, p, 0)
                if here(b + 2):
                    act.wait_ge(s["a_full"], a_turn(*at, "xc"))
                    wait(act, s["s_ok"], 2 * n + 2)
                    if l:
                        act.copy(xT[:, p, :], A[:, 0:P])
                    else:
                        queries(l, p)
                    act.copy(cT[:, p, :], A[:, P:P + NK]).then_inc(s["a_read"], 1)
                if here(b):
                    probs_out(n, p, 1)
                if here(b) or here(b - 2) or here(b - 3):
                    act.wait_ge(s["a_full"], a_turn(*at, "gl"))
                    if here(b):
                        wait(act, s["pv_done"], n)
                        ins = act.copy(RT[:, :], A[:, 2 * P:3 * P])
                    if here(b - 2):
                        ins = act.copy(xgT[:, p, :], A[:, 0:P])
                    if here(b - 3):
                        ins = act.copy(LG[:, (k - 3) % 4, :], A[:, P:P + E])
                    ins.then_inc(s["a_read"], 1)
                if k == 2 and here(b - 6):
                    act.wait_ge(s["r1"], 2 * (4 * l + q - 1) + 2)
                    act.activation(rexp[:, :, :], rsub[:, :, :], ACT.Exp).then_inc(s["rexp_ok"], 1)
                if here(b + 1):
                    exps(n + 1, 1 - p, 0)
                if l and (here(b + 2) or here(b + 1)):
                    act.wait_ge(s["a_full"], a_turn(*at, "qkv"))
                    if here(b + 2):
                        queries(l, p)
                        ins = act.copy(kTs[:, p, :], A[:, P:P + NK])
                    if here(b + 1):
                        wait(act, s["vp_ok"], n)
                        ins = act.copy(Vs[:, 1 - p, :], A[0:NK, 2 * P:3 * P])
                    ins.then_inc(s["a_read"], 1)

            act.wait_ge(s["ident_ok"], 1)
            act.activation(table_load[:, :], minus_half[:, :], ACT.Exp)
            act.wait_ge(s["a_full"], 1)
            act.copy(wfcT[:, :], A[:, 0:P]).then_inc(s["a_read"], 1)
            act.wait_ge(s["q_zero"], 1)
            for l in range(2):
                over_batches(act, l, body)
                act.wait_ge(s["consts_ok"], 1)
                act.wait_ge(s["fill_ok"], l + 1)
                fill_up(act, l, range(1, E, 2))
                if l:
                    act.activation(table_load[:, :], minus_half[:, :], ACT.Gelu)

                def tile(l, r, k, j):
                    m = T0[l] + r
                    if tile_here(l, r + 1):
                        act.wait_ge(s["h_ok"], m + 2)
                        wait(act, s["hT_ok"], m)
                        act.activation(H[:, (k + 1) % 2, 0:FF[l]], S[:, (k + 1) % 2, 0:FF[l]],
                                       ACT.Gelu if l else ACT.Relu).then_inc(s["h_used"], 1)
                    if tile_here(l, r + 2):
                        act.wait_ge(s["xtT_ok"], m + 3)
                        wait(act, s["h_ok"], m + 1)
                        act.copy(xtT[:, k % 2, :], A[:, 0:P]).then_inc(s["xtT_used"], 1)

                over_tiles(act, l, tile, 2, 0)

        @block.tensor
        def _(pe):
            mm = pe.matmul

            def scores(l, b, k, q, h):
                n, p = NB * l + b, k % 2
                pe.wait_ge(s["kb_ok"], n + 1)
                pe.wait_ge(s["bias_ok"], 1)
                wait(pe, s["sub_ok" if h else "exp_ok"], n if h else 2 * n - 1)
                mask = bias1[:, None, :] if l else bias[:, bass.ds(b, 1), :]
                for g in (2 * h, 2 * h + 1):
                    mm(S[:, g, 0:GK], Q[:, p, g, :], KB[:, p, :], start=True, stop=False)
                for g in (2 * h, 2 * h + 1):
                    last = mm(S[:, g, 0:GK].rearrange("p (j k) -> p j k", j=J), identb[:, :],
                              mask.to_broadcast([P, J, NK]), start=False, stop=True)
                last.then_inc(s["s_ok"], 1)

            def probs_t(n, h):
                pe.wait_ge(s["exp_ok"], 2 * n + h + 1)
                for q in range(2):
                    wait(pe, s["pt_used"], 4 * n + 2 * h + q - 1)
                    for j in range(J):
                        at = (q * J + j) * NK
                        t = pe.transpose(PTp[0:NK, q, j * P:(j + 1) * P], PR[:, h, at:at + NK], ident[:, :])
                    t.then_inc(s["pt_ok"], 1)

            def refill(bank_read, t):
                wait(pe, s[bank_read], t - 1)

            def body(l, b, k, q):
                n, p, at = NB * l + b, k % 2, (l, b, k, q)
                if here(b):
                    scores(*at, 1)
                if here(b - 1):
                    pe.wait_ge(s["pt_used"], 4 * n)
                    pe.wait_ge(s["vp_ok"], n)
                    refill("b_read", b_turn(*at, "pv"))
                    for j in range(J):
                        for g in range(G):
                            v = mm(B[32 * g:32 * g + 32, 0:P], VP[:, 1 - p, g, 32 * j:32 * j + 32],
                                   PT[:, 1 - p, (g * J + j) * P:(g * J + j + 1) * P], start=(j == 0), stop=(j == J - 1))
                    v.then_inc(s["b_full"], 1)
                if here(b):
                    probs_t(n, 0)
                if here(b + 2):
                    refill("a_read", a_turn(*at, "xc"))
                    pe.wait_ge(s["xn_ok"], n + 3)
                    pe.wait_ge(ctx_ld[(k + 2) % 4], 16 * (4 * l + q + (k + 2) // 4 + 1))
                    pe.transpose(A[:, 0:P], xn[:, p, :], ident[:, :])
                    pe.transpose(A[:, P:P + NK], ctx[:, (k + 2) % 4, :], ident[0:NK, 0:NK]).then_inc(s["a_full"], 1)
                if here(b + 1):
                    scores(l, b + 1, (k + 1) % 4, q + (k + 1) // 4, 0)
                if here(b):
                    probs_t(n, 1)
                if here(b) or here(b - 2) or here(b - 3):
                    refill("a_read", a_turn(*at, "gl"))
                    if here(b - 2):
                        pe.wait_ge(s["xg_ok"], n - 1)
                    if here(b):
                        pe.wait_ge(s["rx_ok"], n + 1)
                        v = pe.transpose(A[:, 2 * P:3 * P], RX[:, :], ident[:, :])
                    if here(b - 2):
                        v = pe.transpose(A[:, 0:P], xg[:, p, :], ident[:, :])
                    if here(b - 3):
                        pe.wait_ge(s["proj_ld"], 16 * 6)
                        v = mm(A[:, P:P + E], xgT[:, 1 - p, :], gate[l][:, :], start=True, stop=True)
                    v.then_inc(s["a_full"], 1)
                if here(b - 1):
                    refill("b_read", b_turn(*at, "proj"))
                    if l == 0:
                        mm(B[:, 0:D], ones_f[0:1, :], bfc_sb[0:1, :], start=True, stop=False)
                    mm(B[:, 0:D], OT[:, 1 - p, :], wt_sb[:, :] if l else wfcT[:, :],
                       start=bool(l), stop=True).then_inc(s["b_full"], 1)
                if l and (here(b + 2) or here(b + 1)):
                    pe.wait_ge(s["proj_ld"], 16 * 6)
                    refill("a_read", a_turn(*at, "qkv"))
                    if here(b + 2):
                        mm(A[:, 0:P], wq_sb[:, :], xT[:, p, :], start=True, stop=True)
                        v = mm(A[:, P:P + NK], wk_sb[:, :], cT[:, p, :], start=True, stop=True)
                    if here(b + 1):
                        v = mm(A[0:NK, 2 * P:3 * P], cT[:, 1 - p, :], wv_sb[:, :], start=True, stop=True)
                    v.then_inc(s["a_full"], 1)
                if k == 0 and here(b - 8):
                    quad = 4 * l + q - 2
                    pe.wait_ge(s["ohb_ok"], quad + 1)
                    wait(pe, s["consts_ok"], 1)
                    refill("b_read", b_turn(*at, "prefix"))
                    mm(B[:, 0:QT * E], before[:, :], OHB[:, :, :], start=True, stop=False)
                    for d in range(1, QT):
                        mm(B[:, d * E:QT * E], onesb[:, :], OHB[:, 0:QT - d, :], start=False, stop=False)
                    mm(B[:, 0:QT * E].rearrange("p (t e) -> p t e", t=QT), onesb[:, :],
                       OHacc[:, None, :].to_broadcast([P, QT, E]), start=False, stop=True).then_inc(s["b_full"], 1)

            pe.wait_ge(s["wfc_ld"], 32)
            pe.wait_ge(s["ident_ok"], 1)
            pe.transpose(A[:, 0:P], wfc_sb[:, :], ident[:, :]).then_inc(s["a_full"], 1)
            for l in range(2):
                over_batches(pe, l, body)
                pe.wait_ge(s["r3"], R3N[0] * 4 + l * R3N[1] * 4)
                refill("b_read", counts_turn(l))
                mm(B[:, 0:E], onesb[:, :], OHacc[:, :], start=True, stop=True).then_inc(s["b_full"], 1)
                pe.wait_ge(s["tables_ok"], l + 1)
                pe.wait_ge(s["bias_parts"], 16 * 6 * (l + 1))
                pe.wait_ge(s["w_ok"], W_ALL)
                nf = FF[l] // P
                word = [None]

                def expert(word, k, i):
                    return (word >> EBITS * (k + i)) & (E - 1)

                def tile(l, r, k, j):
                    m = T0[l] + r
                    if k == 0 or (isinstance(r, int) and r == -2):
                        word[0] = pe.value_load(TE[l][0:1, bass.ds(j + 1, 1)], min_val=0, max_val=E ** WORD - 1)
                    if tile_here(l, r + 1):
                        e = expert(word[0], k, 2)
                        pe.wait_ge(s["xtT_used"], m + 2)
                        h = S[:, (k + 1) % 2, 0:FF[l]]
                        mm(h, onesb[0:3, :], b1s[l][:, bass.ds(e * FF[l], FF[l])], start=True, stop=False)
                        mm(h, xtT[:, (k + 1) % 2, :], W1[l][:, bass.ds(e * FF[l], FF[l])],
                           start=False, stop=True).then_inc(s["h_ok"], 1)
                    if tile_here(l, r + 2):
                        kk = (k + 2) % 4
                        pe.wait_ge(xt_ld[kk], (j + (k + 2) // 4 + SLOT0[l][kk] + 1) * 16)
                        pe.transpose(A[:, 0:P], xt[:, kk, 0:D], ident[:, :]).then_inc(s["xtT_ok"], 1)
                    if tile_here(l, r):
                        pe.wait_ge(s["h_used"], m + 1)
                        for c in range(nf):
                            v = pe.transpose(S[:, 2 + k % 2, c * P:(c + 1) * P], H[:, k % 2, c * P:(c + 1) * P], ident[:, :])
                        v.then_inc(s["hT_ok"], 1)
                    if tile_here(l, r - 1):
                        e = expert(word[0], k, 0)
                        pe.wait_ge(s["hT_used"], m)
                        wait(pe, s["y_used"], m - 2)
                        y = PTp[:, (k + 1) % 2, 0:D]
                        mm(y, onesb[0:3, :], b2s[l][:, bass.ds(e * D, D)], start=True, stop=False)
                        for c in range(nf):
                            v = mm(y, HT[:, (k + 1) % 2, c * P:(c + 1) * P], W2[l][:, bass.ds(e * FF[l] + c * P, D)],
                                   start=False, stop=(c == nf - 1))
                        v.then_inc(s["y_ok"], 1)

                over_tiles(pe, l, tile, 2, 1)
                done = T0[l] + TILES[l]
                for name in ("hT_used", "h_used", "y_used", "xtT_used"):
                    pe.wait_ge(s[name], done)

        @block.vector
        def _(dve):
            tt, ts, cp = dve.tensor_tensor, dve.tensor_scalar, dve.tensor_copy

            def halves(h):
                return S[:, 2 * h:2 * h + 2, 0:GK].rearrange("p g (j k) -> p g j k", j=J)

            def maximum(n, h):
                dve.wait_ge(s["s_ok"], 2 * n + h + 1)
                if h:
                    wait(dve, s["exp_ok"], 2 * n)
                m = M[:, h, :].rearrange("p (g j) -> p g j", g=2)
                dve.tensor_reduce(m, halves(h), AX_X, ALU.min).then_inc(s["m_ok"], 1)
                if h:
                    dve.wait_ge(s["m_ok"], 2 * n + 2)
                    tt(SB[:, :].rearrange("p (g j k) -> p g j k", g=2, j=J), halves(h),
                       m[:, :, :, None].to_broadcast([P, 2, J, NK]), ALU.subtract).then_inc(s["sub_ok"], 1)

            def recip(n, p):
                dve.wait_ge(s["exp_ok"], 2 * n + 2)
                dve.tensor_reduce(SUM[:, p, 2 * J:NH], PR[:, 1, :].rearrange("p (j k) -> p j k", k=NK),
                                  AX_X, ALU.add).then_inc(s["sum_ok"], 1)
                dve.wait_ge(s["sum_ok"], n + 1)
                dve.reciprocal(R[:, :], SUM[:, p, :]).then_inc(s["recip_ok"], 1)
                dve.wait_ge(s["recip_ok"], n + 1)
                ts(RX[:, :].rearrange("p (h d) -> p h d", d=DH), R[:, :, None].to_broadcast([P, NH, DH]),
                   1.0, None, ALU.mult).then_inc(s["rx_ok"], 1)

            def hold():
                dve.sem_inc(s["held"], 1)

            def stats(src, n, p, k, st, mv, st_ok, mv_ok):
                hold()
                dve.bn_stats(st[:, p, :], src).then_inc(s[st_ok], 1)
                dve.wait_ge(s[st_ok], n + 1)
                hold()
                dve.bn_aggr(mv[:, k, :], st[:, p, :]).then_inc(s[mv_ok], 1)

            def combine(b, k, q):
                dve.wait_ge(gath[k], TOPK[0] * (q + 1) * 16)
                for c in range(2):
                    if c:
                        dve.wait_ge(s["comb_part"], b + 1)
                    dve.scalar_tensor_tensor(out=X[:, b, :], in0=YG[:, k, c, :], scalar=GV[:, c, bass.ds(b, 1)],
                                             in1=X[:, b, :], op0=ALU.mult, op1=ALU.add)\
                        .then_inc(s["combined" if c else "comb_part"], 1)

            def chain(name, base):
                count = [0]

                def link(ins):
                    count[0] += 1
                    ins.then_inc(s[name], 1)
                    dve.wait_ge(s[name], base + count[0])
                return link, count

            def route1(l, quad):
                link, c = chain("r1", quad * R1N)
                link(dve.tensor_reduce(rmax[:, :], LG[:, :, :], AX_X, ALU.max))
                link(tt(rsub[:, :, :], LG[:, :, :], rmax[:, :, None].to_broadcast([P, QT, E]), ALU.subtract))
                assert c[0] == R1N

            def over_e(v):
                return v[:, :, None].to_broadcast([P, QT, E])

            def route2(l, quad, t0, part):
                starts = (0, 3, 6, 9, 12, 14) if TOPK[l] == 2 else (0, 3, 6, 6, 6, 8)
                start, stop = starts[part:part + 2]
                link, c = chain("r2", (quad * R2N[l] if l == 0 else (quad - 4) * R2N[1] + 4 * R2N[0]) + start)

                def oh(k):
                    return OH[:, k, bass.ds(t0, QT), :]

                def best(k, pk):
                    link(dve.tensor_reduce(val[:, k, :], pk[:, :, :], AX_X, ALU.max))
                    link(tt(eq[:, :, :], pk[:, :, :], over_e(val[:, k, :]), ALU.is_equal))
                    link(tt(rank[:, :, :], eq[:, :, :], revf[:, :, :], ALU.mult))

                def chosen(k):
                    link(dve.tensor_reduce(first[:, :], rank[:, :, :], AX_X, ALU.max))
                    link(tt(oh(k), revf[:, :, :], over_e(first), ALU.is_equal))

                if part == 0:
                    dve.wait_ge(s["rexp_ok"], quad + 1)
                    dve.wait_ge(s["consts_ok"], 1)
                    link(dve.tensor_reduce(rsum[:, :], rexp[:, :, :], AX_X, ALU.add))
                    link(dve.reciprocal(rrec[:, :], rsum[:, :]))
                    link(tt(prob[:, :, :], rexp[:, :, :], over_e(rrec), ALU.mult))
                if part == 1:
                    best(0, prob)
                if part == 2 and TOPK[l] == 2:
                    chosen(0)
                    link(dve.scalar_tensor_tensor(out=prob2[:, :, :], in0=oh(0), scalar=-2.0,
                                                  in1=prob[:, :, :], op0=ALU.mult, op1=ALU.add))
                if part == 3 and TOPK[l] == 2:
                    best(1, prob2)
                if part == 4 and TOPK[l] == 2:
                    chosen(1)
                    tt(OHB[:, :, :], oh(0), oh(1), ALU.add).then_inc(s["ohb_ok"], 1)
                if part == 4 and TOPK[l] == 1:
                    chosen(0)
                    ts(OHB[:, :, :], oh(0), 1.0, None, ALU.mult).then_inc(s["ohb_ok"], 1)
                assert start + c[0] == stop, c

            def route3(l, quad, t0, turn_no):
                link, c = chain("r3", quad * R3N[0] if l == 0 else (quad - 4) * R3N[1] + 4 * R3N[0])
                dve.wait_ge(s["b_full"], turn_no)
                tt(pos[:, :, :], B[:, 0:QT * E].rearrange("p (t e) -> p t e", t=QT), region0[:, :, :],
                   ALU.add).then_inc(s["b_read"], 1)
                dve.wait_ge(s["b_read"], turn_no)
                if TOPK[l] == 1:
                    link(ts(XR[:, bass.ds(t0, QT), 2 * D], val[:, 0, :], 1.0, None, ALU.mult))
                kk = TOPK[l]
                link(tt(posk[:, 0:kk, :, :], pos[:, None, :, :].to_broadcast([P, kk, QT, E]), OH[:, 0:kk, bass.ds(t0, QT), :],
                        ALU.mult))
                link(dve.tensor_reduce(POSF[:, 0:kk, bass.ds(t0, QT)], posk[:, 0:kk, :, :], AX_X, ALU.add))
                ts(IDX[l][:, 0:kk, bass.ds(t0, QT)], POSF[:, 0:kk, bass.ds(t0, QT)], 1.0, None, ALU.mult)\
                    .then_inc(s["idx_ok"], 1)
                link(dve.tensor_reduce(ohsum[:, :], OHB[:, :, :].rearrange("p t e -> p e t"), AX_X, ALU.add))
                link(tt(OHacc[:, :], OHacc[:, :], ohsum[:, :], ALU.add))
                if TOPK[l] == 2:
                    link(tt(gden[:, :], val[:, 0, :], val[:, 1, :], ALU.add))
                    link(ts(gden[:, :], gden[:, :], 1e-12, None, ALU.max))
                    link(dve.reciprocal(gden[:, :], gden[:, :]))
                    link(tt(GV[:, :, bass.ds(t0, QT)], val[:, :, :], gden[:, None, :].to_broadcast([P, 2, QT]), ALU.mult))
                dve.wait_ge(s["idx_ok"], quad + 1)
                assert c[0] == R3N[l], c

            def keys(n, p, l, t):
                dve.wait_ge(s["a_read"], t)
                wait(dve, s["s_ok"], 2 * n + 2)
                src = kTs if l else cT
                tt(KB[:, p, :].rearrange("p (j k) -> p j k", j=J), src[:, p, None, :].to_broadcast([P, J, NK]),
                   own[:, :, None].to_broadcast([P, J, NK]), ALU.mult).then_inc(s["kb_ok"], 1)

            def row(t):
                return X[:, bass.ds(t, 1), :].rearrange("p a d -> p (a d)")

            def attended(l, t):
                return XR[:, bass.ds(t, 1), D:2 * D].rearrange("p a d -> p (a d)") if l else row(t)

            def body(l, b, k, q):
                n, p, at = NB * l + b, k % 2, (l, b, k, q)
                if here(b + 2):
                    kk = (k + 2) % 4
                    dve.wait_ge(s["rstd1_ok"], n + 3)
                    ts(xn[:, p, :], row(b + 2), mv1[:, kk, 0:1], rstd1[:, kk:kk + 1],
                       ALU.subtract, ALU.mult).then_inc(s["xn_ok"], 1)
                if here(b):
                    maximum(n, 1)
                if here(b + 1) and l:
                    keys(n - 1, 1 - p, l, a_turn(l, b - 1, (k - 1) % 4, q - (k == 0), "qkv"))
                if here(b - 1):
                    dve.wait_ge(s["b_full"], b_turn(*at, "pv"))
                    dve.wait_ge(s["a_read"], a_turn(l, b - 1, (k - 1) % 4, q - (k == 0), "gl"))
                    tt(OT[:, 1 - p, :], B[:, 0:P], RT[:, :], ALU.mult).then_inc(s["b_read"], 1)
                    dve.sem_inc(s["pv_done"], 1)
                if k == 3 and here(b - 7):
                    route2(l, 4 * l + q - 1, (q - 1) * QT, 1)
                if k == 0 and here(b - 8):
                    route2(l, 4 * l + q - 2, (q - 2) * QT, 4)
                if here(b):
                    recip(n, p)
                if here(b - 2):
                    dve.wait_ge(s["rstd2_ok"], n - 1)
                    if here(b - 4) and not here(b + 1):
                        dve.wait_ge(s["a_full"], a_turn(l, b - 2, (k - 2) % 4, q - (k < 2), "gl"))
                    kk = (k - 2) % 4
                    ts(xg[:, p, :], attended(l, b - 2), mv2[:, kk, 0:1], rstd2[:, kk:kk + 1],
                       ALU.subtract, ALU.mult).then_inc(s["xg_ok"], 1)
                if here(b + 1):
                    maximum(n + 1, 0)
                if k == 3 and here(b - 7):
                    route2(l, 4 * l + q - 1, (q - 1) * QT, 2)
                if k == 2 and here(b - 6):
                    dve.wait_ge(s["a_read"], a_turn(*at, "gl"))
                    route1(l, 4 * l + q - 1)
                if here(b + 2) and not l:
                    keys(n, p, l, a_turn(*at, "xc"))
                if here(b + 3):
                    kk = (k + 3) % 4
                    if l:
                        combine(b + 3, kk, q + (k + 3) // 4)
                        dve.wait_ge(s["combined"], b + 4)
                    else:
                        dve.wait_ge(x_ld[0], 16)
                        if not isinstance(b, int) or b + 3 >= 4:
                            dve.wait_ge(x_ld[1], 16)
                    stats(row(b + 3), n + 3, 1 - p, kk, st1, mv1, "st1_ok", "mv1_ok")
                if here(b - 1):
                    dve.wait_ge(s["b_full"], b_turn(*at, "proj"))
                    xb = attended(l, b - 1)
                    tt(xb, B[:, 0:D], row(b - 1), ALU.add).then_inc(s["b_read"], 1)
                    dve.wait_ge(s["b_read"], b_turn(*at, "proj"))
                    wait(dve, s["xn2_ok"], n - 4)
                    stats(xb, n - 1, 1 - p, (k - 1) % 4, st2, mv2, "st2_ok", "mv2_ok")
                if l == 0 and isinstance(b, int) and b == -2:
                    dve.wait_ge(s["mask_ld"], 32)
                    ts(bias1[:, :], mask1_sb[:, :], 0.0, MASKED, ALU.is_equal, ALU.mult)
                    ts(bias[:, :, :], mask0_sb[:, :, :], 0.0, MASKED, ALU.is_equal, ALU.mult).then_inc(s["bias_ok"], 1)
                if k == 2 and here(b - 6):
                    route2(l, 4 * l + q - 1, (q - 1) * QT, 0)
                if k == 3 and here(b - 7):
                    route2(l, 4 * l + q - 1, (q - 1) * QT, 3)
                if k == 0 and here(b - 8):
                    route3(l, 4 * l + q - 2, (q - 2) * QT, b_turn(*at, "prefix"))

            def tables(l):
                link, c = chain("tab", l * TABN[0])

                def experts(i, nw):
                    return tef[:, i:i + 4 * nw].rearrange("p (w t) -> p w t", t=4)[:, :, 0]
                nt = TILES[l]
                dve.wait_ge(s["b_full"], counts_turn(l))
                cp(cnt[:, :], B[:, 0:E]).then_inc(s["b_read"], 1)
                dve.wait_ge(s["b_read"], counts_turn(l))
                link(tt(fillf[:, :], cnt[0:1, :], region0[0:1, 0, :], ALU.add))
                cp(FILL[l][:, :], fillf[:, :]).then_inc(s["fill_ok"], 1)
                link(ts(cnti[:, :], cnt[:, :], float(P - 1), None, ALU.add))
                link(ts(nti[:, :], cnti[:, :], 7, None, ALU.arith_shift_right))
                link(cp(ntf[:, :], nti[:, :]))
                link(cp(cum[:, 0, 4:], nti[:, :]))
                for i, d in enumerate((1, 2, 4)):
                    link(tt(cum[:, i + 1, 4:], cum[:, i, 4:], cum[:, i, 4 - d:4 + E - d], ALU.add))
                total = cum[0:1, 3, 3 + E:4 + E]
                shape = [1, nt, E - 1]
                link(tt(ge[:, 0:nt, :], tile_no[:, 0:nt, :], cum[0:1, 3, None, 4:3 + E].to_broadcast(shape), ALU.is_ge))
                link(dve.tensor_reduce(tef[:, WORD - 1:WORD - 1 + nt], ge[:, 0:nt, :], AX_X, ALU.add))
                link(tt(gen[:, 0:nt, :], ge[:, 0:nt, :], ntf[0:1, None, 0:E - 1].to_broadcast(shape), ALU.mult))
                link(dve.tensor_reduce(startf[:, 0:nt], gen[:, 0:nt, :], AX_X, ALU.add))
                link(ts(validf[:, 0:nt], tile_no[:, 0:nt, 0], total, None, ALU.is_lt))
                link(tt(offf[:, 0:nt], tile_no[:, 0:nt, 0], startf[:, 0:nt], ALU.subtract))
                link(dve.scalar_tensor_tensor(out=offf[:, 0:nt], in0=offf[:, 0:nt], scalar=float(P), in1=validf[:, 0:nt],
                                              op0=ALU.mult, op1=ALU.mult))
                link(tt(tel[:, 0:nt], tef[:, WORD - 1:WORD - 1 + nt], validf[:, 0:nt], ALU.subtract))
                link(dve.scalar_tensor_tensor(out=rowf[:, 0:nt], in0=tel[:, 0:nt], scalar=float(REGION), in1=offf[:, 0:nt],
                                              op0=ALU.mult, op1=ALU.add))
                ts(ROW[l][:, :], rowf[:, 0:nt], float(REGION), None, ALU.add)
                nw = NW[l]
                link(cp(packf[:, 0:nw], experts(WORD - 1, nw)))
                for i in range(WORD - 2, -1, -1):
                    link(dve.scalar_tensor_tensor(out=packf[:, 0:nw], in0=packf[:, 0:nw], scalar=float(E),
                                                  in1=experts(i, nw), op0=ALU.mult, op1=ALU.add))
                cp(TE[l][:, :], packf[:, 0:nw]).then_inc(s["tables_ok"], 1)
                link(dve.memset(OHacc[:, :], 0.0))
                if l == 0:
                    link(tt(shift[:, :], cum[:, 3, 4:], ntf[:, :], ALU.subtract))
                    link(dve.scalar_tensor_tensor(out=shift[:, :], in0=shift[:, :], scalar=float(P), in1=region0[:, 0, :],
                                                  op0=ALU.mult, op1=ALU.subtract))
                    link(tt(moved[:, :, :], OH[:, :, :, :].rearrange("p k t e -> p (k t) e"),
                            shift[:, None, :].to_broadcast([P, 2 * NB, E]), ALU.mult))
                    link(dve.tensor_reduce(movedr[:, :], moved[:, :, :], AX_X, ALU.add))
                    link(tt(movedr[:, :], movedr[:, :], POSF[:, :, :].rearrange("p k t -> p (k t)"), ALU.add))
                    link(cp(IDXG[:, :, :].rearrange("p k t -> p (k t)"), movedr[:, :]))
                dve.sem_inc(s["idxg_ok"], 1)
                assert c[0] == TABN[l], c

            for l in range(2):
                over_batches(dve, l, body)
                tables(l)

                def tile(l, r, k, j):
                    m = T0[l] + r
                    if tile_here(l, r):
                        dve.wait_ge(s["hT_ok"], m + 1)
                        wait(dve, s["y_ok"], m - 1)
                        cp(HT[:, k % 2, 0:FF[l]], S[:, 2 + k % 2, 0:FF[l]]).then_inc(s["hT_used"], 1)
                    if tile_here(l, r - 1):
                        kk = (k - 1) % 4
                        dve.wait_ge(s["y_ok"], m)
                        wait(dve, out_st[kk] if l else y_st[kk], (j + (k - 1) // 4) * 16)
                        if l:
                            cp(Ytok[:, kk:kk + 1], carried[:, kk, D + 1:])
                            dve.scalar_tensor_tensor(out=Y[:, kk, :], in0=PTp[:, kk % 2, 0:D], scalar=carried[:, kk, D:D + 1],
                                                     in1=carried[:, kk, 0:D], op0=ALU.mult, op1=ALU.add)\
                                .then_inc(s["y_used"], 1)
                        else:
                            cp(Y[:, kk, :], PTp[:, kk % 2, 0:D]).then_inc(s["y_used"], 1)

                    if l and tile_here(l, r + 2):
                        kk = (k + 2) % 4
                        dve.wait_ge(s["xtT_ok"], m + 3)
                        dve.wait_ge(s["y_used"], m - 1)
                        cp(carried[:, kk, :], xt[:, kk, D:]).then_inc(s["carried_ok"], 1)

                over_tiles(dve, l, tile, 2, 1)


_INS = ['x', 'ctx_1024', 'mask_Bx1xSxS2_ik1', 'mask_1x1xSxS2_if1', 'L0_xattn_W_fc', 'L0_xattn_b_fc', 'L0_ffn_gate',
        'L0_ffn_W1', 'L0_ffn_b1', 'L0_ffn_W2', 'L0_ffn_b2', 'L1_xattn_W_Q', 'L1_xattn_W_K', 'L1_xattn_W_V',
        'L1_xattn_W_T', 'L1_ffn_gate_w', 'L1_ffn_w1', 'L1_ffn_b1', 'L1_ffn_w2', 'L1_ffn_b2']


def kernel(**inputs):
    import numpy as _np
    import concourse.bacc as _bacc
    from concourse import mybir as _mybir
    from concourse.bass_utils import run_bass_kernel_spmd as _run

    nc = _bacc.Bacc("TRN2", target_bir_lowering=False, num_devices=1)
    arrays, args = {}, []
    for name in _INS:
        a = _np.ascontiguousarray(inputs[name])
        arrays[f"in_{name}_dram"] = a
        args.append(nc.dram_tensor(f"in_{name}_dram", a.shape, _mybir.dt.from_np(a.dtype), kind="ExternalInput").ap())
    args.append(nc.dram_tensor("out_dram", (16, 128, 128), _mybir.dt.float32, kind="ExternalOutput").ap())
    build(nc, *args)
    r = _run(nc, [arrays], core_ids=[0])
    return r.results[0]["out_dram"]
```
